# Optimizing a Trainium2 kernel written in Bass

```python
import numpy as np
import jax
import jax.numpy as jnp

def _softmax(x, axis=-1):
    return jax.nn.softmax(x, axis=axis)

def _gelu(x):
    return jax.nn.gelu(x, approximate=True)

def _silu(x):
    return jax.nn.silu(x)

def _sigmoid(x):
    return jax.nn.sigmoid(x)

def _layernorm(x, axis=-1, eps=1e-05):
    m = jnp.mean(x, axis=axis, keepdims=True)
    v = jnp.var(x, axis=axis, keepdims=True)
    return (x - m) / jnp.sqrt(v + eps)

def _scatter_add(tgt, idx, src, axis=0):
    return tgt.at[idx].add(src)

def _segment_sum(src, seg, n):
    return jax.ops.segment_sum(src, seg, n)
kernel_name = 'mk_xattn_ffn_d4_seqx_r8_33ede9'

def setup_inputs(seed: int=0):
    np.random.seed(seed)
    _w = jnp.asarray

    def _rec_inputs():
        import jax
        import jax.numpy as jnp
        _rk = jax.random.key(seed)
        x = -0.0002928 + 1 * jax.random.normal(jax.random.fold_in(_rk, 1), (4, 512, 128), jnp.float32)
        _lenS = 512 - jax.random.randint(jax.random.fold_in(_rk, 7), (4,), 0, max(1, 512 // 4) + 1, jnp.int32)
        _lenS2 = 77 - jax.random.randint(jax.random.fold_in(_rk, 8), (4,), 0, max(1, 77 // 4) + 1, jnp.int32)
        _ctx_1024P = jax.random.normal(jax.random.fold_in(_rk, 11), (4, 16, 128), jnp.float32)
        _ctx_1024c = jax.random.dirichlet(jax.random.fold_in(_rk, 511), 0.3 * jnp.ones((16,), jnp.float32), (4, 77))
        _ctx_1024t = jnp.einsum('bsk,bkd->bsd', _ctx_1024c, _ctx_1024P)
        _ctx_1024t = _ctx_1024t * jax.lax.rsqrt(jnp.mean(jnp.square(_ctx_1024t)) + 1e-12) * 0.953939
        ctx_1024 = -1.39393e-06 + 0.999914 * (_ctx_1024t + 0.3 * jax.random.normal(jax.random.fold_in(_rk, 611), (4, 77, 128), jnp.float32))
        return (x, ctx_1024)
    x, ctx_1024 = _rec_inputs()

    def _L0_xattn_setup():
        import jax, jax.numpy as jnp
        import numpy as np
        HEAD = 16
        D = 128
        DK = D // HEAD
        key = jax.random.key(seed)
        ks = jax.random.split(key, 11)
        B, S = (2, 256)
        scale = 1.0 / np.sqrt(D)
        inp = {'query': jax.random.normal(ks[0], (B, S, D), jnp.float32), 'key_in': jax.random.normal(ks[1], (B, S, D), jnp.float32), 'value': jax.random.normal(ks[2], (B, S, D), jnp.float32), 'Wq': jax.random.normal(ks[3], (D, D), jnp.float32) * scale, 'bq': jnp.zeros((D,), jnp.float32), 'Wk': jax.random.normal(ks[4], (D, D), jnp.float32) * scale, 'bk': jnp.zeros((D,), jnp.float32), 'Wv': jax.random.normal(ks[5], (D, D), jnp.float32) * scale, 'bv': jnp.zeros((D,), jnp.float32), 'Wo': jax.random.normal(ks[6], (D, D), jnp.float32) * scale, 'bo': jnp.zeros((D,), jnp.float32)}
        return inp
    _L0_xattn_all = _L0_xattn_setup()
    _L0_xattn_in = {k: v for k, v in _L0_xattn_all.items() if k in ('Wq', 'bq', 'Wk', 'bk', 'Wv', 'bv', 'Wo', 'bo')}
    del _L0_xattn_all

    def _L0_ffn_setup():
        import jax, jax.numpy as jnp
        import numpy as np
        B, L, D = (4, 64, 128)
        E, TOP_K = (16, 4)
        F = 4 * D
        key = jax.random.key(seed)
        ks = jax.random.split(key, 6)
        scale = 0.02
        return {'x': jax.random.normal(ks[0], (B, L, D), jnp.float32), 'keys': jax.random.normal(ks[1], (E, D), jnp.float32), 'w1': jax.random.normal(ks[2], (E, F, D), jnp.float32) * scale, 'b1': jnp.zeros((E, F), jnp.float32), 'w2': jax.random.normal(ks[3], (E, D, F), jnp.float32) * scale, 'b2': jnp.zeros((E, D), jnp.float32), 'rw': jax.random.normal(ks[4], (E, D), jnp.float32) * scale, 'rb': jnp.zeros((E,), jnp.float32)}
    _L0_ffn_all = _L0_ffn_setup()
    _L0_ffn_in = {k: v for k, v in _L0_ffn_all.items() if k in ('keys', 'w1', 'b1', 'w2', 'b2', 'rw', 'rb')}
    del _L0_ffn_all

    def _L1_xattn_setup():
        import jax, jax.numpy as jnp
        import numpy as np
        DIM = 128
        NUM_HEADS = 16
        DIM_HEAD = 64
        INNER = NUM_HEADS * DIM_HEAD
        SCALE = DIM_HEAD ** (-0.5)

        def _layernorm(x, gamma, beta, eps=1e-05):
            mu = jnp.mean(x, axis=-1, keepdims=True)
            var = jnp.mean(jnp.square(x - mu), axis=-1, keepdims=True)
            return (x - mu) * jax.lax.rsqrt(var + eps) * gamma + beta
        key = jax.random.key(seed)
        ks = jax.random.split(key, 8)
        B, SQ, SK = (2, 256, 512)
        x = jax.random.normal(ks[0], (B, SQ, DIM), dtype=jnp.float32)
        context = jax.random.normal(ks[1], (B, SK, DIM), dtype=jnp.float32)
        ln_gamma = jnp.ones((DIM,), jnp.float32)
        ln_beta = jnp.zeros((DIM,), jnp.float32)
        w_q = jax.random.normal(ks[2], (DIM, INNER), dtype=jnp.float32) / np.sqrt(DIM)
        w_kv = jax.random.normal(ks[3], (DIM, 2 * INNER), dtype=jnp.float32) / np.sqrt(DIM)
        w_out = jax.random.normal(ks[4], (INNER, DIM), dtype=jnp.float32) / np.sqrt(INNER)
        b_out = jnp.zeros((DIM,), jnp.float32)
        gate = jnp.array([0.5], jnp.float32)
        return {'x': x, 'context': context, 'ln_gamma': ln_gamma, 'ln_beta': ln_beta, 'w_q': w_q, 'w_kv': w_kv, 'w_out': w_out, 'b_out': b_out, 'gate': gate}
    _L1_xattn_all = _L1_xattn_setup()
    _L1_xattn_in = {k: v for k, v in _L1_xattn_all.items() if k in ('ln_gamma', 'ln_beta', 'w_q', 'w_kv', 'w_out', 'b_out', 'gate')}
    del _L1_xattn_all

    def _L1_ffn_setup():
        import jax, jax.numpy as jnp
        import numpy as np
        NUM_EXPERTS = 8
        EXPERT_CAPACITY = 2.0
        DIM = 128
        HIDDEN_DIM = 512
        key = jax.random.key(seed)
        k_x, k_g, k_w1, k_w2 = jax.random.split(key, 4)
        n, t, d, f, e = (8, 128, DIM, HIDDEN_DIM, NUM_EXPERTS)
        x = jax.random.normal(k_x, (n, t, d), dtype=jnp.float32)
        gate_w = jax.random.normal(k_g, (e, d), dtype=jnp.float32) * 0.02
        w1 = jax.random.normal(k_w1, (e, d, f), dtype=jnp.float32) * 0.02
        w2 = jax.random.normal(k_w2, (e, f, d), dtype=jnp.float32) * 0.02
        return {'x': x, 'gate_w': gate_w, 'w1': w1, 'w2': w2}
    _L1_ffn_all = _L1_ffn_setup()
    _L1_ffn_in = {k: v for k, v in _L1_ffn_all.items() if k in ('gate_w', 'w1', 'w2')}
    del _L1_ffn_all

    def _L2_xattn_setup():
        import jax, jax.numpy as jnp
        import numpy as np
        import math
        D_MODEL = 128
        N_HEADS = 16
        HEAD_DIM = D_MODEL // N_HEADS
        TOP_K = 32
        SCALE = math.sqrt(HEAD_DIM)

        def _split_heads(t, n):
            B, L, _ = t.shape
            return t.reshape(B, L, N_HEADS, HEAD_DIM).transpose(0, 2, 1, 3)
        key = jax.random.key(seed)
        ks = jax.random.split(key, 12)
        B, S, N = (2, 256, 256)
        std = 1.0 / math.sqrt(D_MODEL)
        inp = {'x': jax.random.normal(ks[0], (B, S, D_MODEL), dtype=jnp.float32), 'knowledge_embeddings': jax.random.normal(ks[1], (B, N, D_MODEL), dtype=jnp.float32), 'Wq': jax.random.normal(ks[2], (D_MODEL, D_MODEL), dtype=jnp.float32) * std, 'bq': jnp.zeros((D_MODEL,), dtype=jnp.float32), 'Wk': jax.random.normal(ks[3], (D_MODEL, D_MODEL), dtype=jnp.float32) * std, 'bk': jnp.zeros((D_MODEL,), dtype=jnp.float32), 'Wv': jax.random.normal(ks[4], (D_MODEL, D_MODEL), dtype=jnp.float32) * std, 'bv': jnp.zeros((D_MODEL,), dtype=jnp.float32), 'Wo': jax.random.normal(ks[5], (D_MODEL, D_MODEL), dtype=jnp.float32) * std, 'bo': jnp.zeros((D_MODEL,), dtype=jnp.float32)}
        return inp
    _L2_xattn_all = _L2_xattn_setup()
    _L2_xattn_in = {k: v for k, v in _L2_xattn_all.items() if k in ('Wq', 'bq', 'Wk', 'bk', 'Wv', 'bv', 'Wo', 'bo')}
    del _L2_xattn_all

    def _L2_ffn_setup():
        import jax, jax.numpy as jnp
        import numpy as np
        B, T, DIM, H, DH, TOPK = (4, 256, 128, 8, 64, 3)
        key = jax.random.key(seed)
        ks = jax.random.split(key, 6)
        x = jax.random.normal(ks[0], (B, T, DIM), dtype=jnp.float32)
        sc = 1.0 / np.sqrt(DIM)
        Wq = jax.random.normal(ks[1], (DIM, H * DH), dtype=jnp.float32) * sc
        Wkv = jax.random.normal(ks[2], (DIM, 2 * H * DH), dtype=jnp.float32) * sc
        Ws = jax.random.normal(ks[3], (DIM, H), dtype=jnp.float32) * sc
        Wo = jax.random.normal(ks[4], (H, DH, DIM), dtype=jnp.float32) * (1.0 / np.sqrt(DH))
        bo = jax.random.normal(ks[5], (H, DIM), dtype=jnp.float32) * 0.01
        return {'x': x, 'Wq': Wq, 'Wkv': Wkv, 'Ws': Ws, 'Wo': Wo, 'bo': bo}
    _L2_ffn_all = _L2_ffn_setup()
    _L2_ffn_in = {k: v for k, v in _L2_ffn_all.items() if k in ('Wq', 'Wkv', 'Ws', 'Wo', 'bo')}
    del _L2_ffn_all

    def _L3_xattn_setup():
        import jax, jax.numpy as jnp
        import numpy as np
        QUERY_DIM = 128
        CONTEXT_DIM = 128
        HEADS = 8
        DIM_HEAD = 64
        INNER = HEADS * DIM_HEAD
        SCALE = DIM_HEAD ** (-0.5)
        key = jax.random.key(seed)
        ks = jax.random.split(key, 7)
        B, N, M = (2, 256, 256)
        x = jax.random.normal(ks[0], (B, N, QUERY_DIM), dtype=jnp.float32)
        context = jax.random.normal(ks[1], (B, M, CONTEXT_DIM), dtype=jnp.float32)
        Wq = jax.random.normal(ks[2], (QUERY_DIM, INNER), dtype=jnp.float32) * QUERY_DIM ** (-0.5)
        Wk = jax.random.normal(ks[3], (CONTEXT_DIM, INNER), dtype=jnp.float32) * CONTEXT_DIM ** (-0.5)
        Wv = jax.random.normal(ks[4], (CONTEXT_DIM, INNER), dtype=jnp.float32) * CONTEXT_DIM ** (-0.5)
        Wo = jax.random.normal(ks[5], (INNER, QUERY_DIM), dtype=jnp.float32) * INNER ** (-0.5)
        bo = jax.random.normal(ks[6], (QUERY_DIM,), dtype=jnp.float32) * 0.01
        return {'x': x, 'context': context, 'Wq': Wq, 'Wk': Wk, 'Wv': Wv, 'Wo': Wo, 'bo': bo}
    _L3_xattn_all = _L3_xattn_setup()
    _L3_xattn_in = {k: v for k, v in _L3_xattn_all.items() if k in ('Wq', 'Wk', 'Wv', 'Wo', 'bo')}
    del _L3_xattn_all

    def _L3_ffn_setup():
        import jax, jax.numpy as jnp
        import numpy as np
        EPS = 1e-05

        def _quantize(W):
            gamma = jnp.mean(jnp.abs(W))
            return jnp.clip(jnp.round(W / (gamma + EPS)), -1.0, 1.0)
        key = jax.random.key(seed)
        k_x, k_w1, k_b1, k_w2, k_b2 = jax.random.split(key, 5)
        n_embd = 128
        d_ff = 4 * n_embd
        B, S = (4, 512)
        bound1 = 1.0 / np.sqrt(n_embd)
        bound2 = 1.0 / np.sqrt(d_ff)
        x = jax.random.normal(k_x, (B, S, n_embd), dtype=jnp.float32)
        W1 = jax.random.uniform(k_w1, (d_ff, n_embd), jnp.float32, -bound1, bound1)
        b1 = jax.random.uniform(k_b1, (d_ff,), jnp.float32, -bound1, bound1)
        W2 = jax.random.uniform(k_w2, (n_embd, d_ff), jnp.float32, -bound2, bound2)
        b2 = jax.random.uniform(k_b2, (n_embd,), jnp.float32, -bound2, bound2)
        return {'x': x, 'W1': W1, 'b1': b1, 'W2': W2, 'b2': b2}
    _L3_ffn_all = _L3_ffn_setup()
    _L3_ffn_in = {k: v for k, v in _L3_ffn_all.items() if k in ('W1', 'b1', 'W2', 'b2')}
    del _L3_ffn_all
    return {'x': x, 'ctx_1024': ctx_1024, 'L0_xattn_Wq': _L0_xattn_in['Wq'], 'L0_xattn_bq': _L0_xattn_in['bq'], 'L0_xattn_Wk': _L0_xattn_in['Wk'], 'L0_xattn_bk': _L0_xattn_in['bk'], 'L0_xattn_Wv': _L0_xattn_in['Wv'], 'L0_xattn_bv': _L0_xattn_in['bv'], 'L0_xattn_Wo': _L0_xattn_in['Wo'], 'L0_xattn_bo': _L0_xattn_in['bo'], 'L0_ffn_keys': _L0_ffn_in['keys'], 'L0_ffn_w1': _L0_ffn_in['w1'], 'L0_ffn_b1': _L0_ffn_in['b1'], 'L0_ffn_w2': _L0_ffn_in['w2'], 'L0_ffn_b2': _L0_ffn_in['b2'], 'L0_ffn_rw': _L0_ffn_in['rw'], 'L0_ffn_rb': _L0_ffn_in['rb'], 'L1_xattn_ln_gamma': _L1_xattn_in['ln_gamma'], 'L1_xattn_ln_beta': _L1_xattn_in['ln_beta'], 'L1_xattn_w_q': _L1_xattn_in['w_q'], 'L1_xattn_w_kv': _L1_xattn_in['w_kv'], 'L1_xattn_w_out': _L1_xattn_in['w_out'], 'L1_xattn_b_out': _L1_xattn_in['b_out'], 'L1_xattn_gate': _L1_xattn_in['gate'], 'L1_ffn_gate_w': _L1_ffn_in['gate_w'], 'L1_ffn_w1': _L1_ffn_in['w1'], 'L1_ffn_w2': _L1_ffn_in['w2'], 'L2_xattn_Wq': _L2_xattn_in['Wq'], 'L2_xattn_bq': _L2_xattn_in['bq'], 'L2_xattn_Wk': _L2_xattn_in['Wk'], 'L2_xattn_bk': _L2_xattn_in['bk'], 'L2_xattn_Wv': _L2_xattn_in['Wv'], 'L2_xattn_bv': _L2_xattn_in['bv'], 'L2_xattn_Wo': _L2_xattn_in['Wo'], 'L2_xattn_bo': _L2_xattn_in['bo'], 'L2_ffn_Wq': _L2_ffn_in['Wq'], 'L2_ffn_Wkv': _L2_ffn_in['Wkv'], 'L2_ffn_Ws': _L2_ffn_in['Ws'], 'L2_ffn_Wo': _L2_ffn_in['Wo'], 'L2_ffn_bo': _L2_ffn_in['bo'], 'L3_xattn_Wq': _L3_xattn_in['Wq'], 'L3_xattn_Wk': _L3_xattn_in['Wk'], 'L3_xattn_Wv': _L3_xattn_in['Wv'], 'L3_xattn_Wo': _L3_xattn_in['Wo'], 'L3_xattn_bo': _L3_xattn_in['bo'], 'L3_ffn_W1': _L3_ffn_in['W1'], 'L3_ffn_b1': _L3_ffn_in['b1'], 'L3_ffn_W2': _L3_ffn_in['W2'], 'L3_ffn_b2': _L3_ffn_in['b2']}

def reference(x, ctx_1024, L0_xattn_Wq, L0_xattn_bq, L0_xattn_Wk, L0_xattn_bk, L0_xattn_Wv, L0_xattn_bv, L0_xattn_Wo, L0_xattn_bo, L0_ffn_keys, L0_ffn_w1, L0_ffn_b1, L0_ffn_w2, L0_ffn_b2, L0_ffn_rw, L0_ffn_rb, L1_xattn_ln_gamma, L1_xattn_ln_beta, L1_xattn_w_q, L1_xattn_w_kv, L1_xattn_w_out, L1_xattn_b_out, L1_xattn_gate, L1_ffn_gate_w, L1_ffn_w1, L1_ffn_w2, L2_xattn_Wq, L2_xattn_bq, L2_xattn_Wk, L2_xattn_bk, L2_xattn_Wv, L2_xattn_bv, L2_xattn_Wo, L2_xattn_bo, L2_ffn_Wq, L2_ffn_Wkv, L2_ffn_Ws, L2_ffn_Wo, L2_ffn_bo, L3_xattn_Wq, L3_xattn_Wk, L3_xattn_Wv, L3_xattn_Wo, L3_xattn_bo, L3_ffn_W1, L3_ffn_b1, L3_ffn_W2, L3_ffn_b2):
    import jax
    import jax.numpy as jnp

    def _L0_xattn_ref(query, key_in, value, Wq, bq, Wk, bk, Wv, bv, Wo, bo):
        import jax, jax.numpy as jnp
        import numpy as np
        HEAD = 16
        D = 128
        DK = D // HEAD
        B, S, _ = query.shape

        def proj(x, W, b):
            return (x @ W.T + b).reshape(B, -1, HEAD, DK).transpose(0, 2, 1, 3)
        q = proj(query, Wq, bq)
        k = proj(key_in, Wk, bk)
        v = proj(value, Wv, bv)
        scores = jnp.einsum('bhqd,bhkd->bhqk', q, k) / jnp.sqrt(jnp.float32(DK))
        attn = jax.nn.softmax(scores, axis=-1)
        x = jnp.einsum('bhqk,bhkd->bhqd', attn, v)
        x = x.transpose(0, 2, 1, 3).reshape(B, S, HEAD * DK)
        return x @ Wo.T + bo

    def _L0_ffn_ref(x, keys, w1, b1, w2, b2, rw, rb):
        import jax, jax.numpy as jnp
        import numpy as np
        B, L, D = (4, 64, 128)
        E, TOP_K = (16, 4)
        F = 4 * D
        diff = x[:, :, None, :] - keys
        dist2 = jnp.sum(diff * diff, axis=-1)
        logits = -dist2 + jnp.einsum('bld,ed->ble', x, rw) + rb
        topv, topi = jax.lax.top_k(logits, TOP_K)
        w = jax.nn.softmax(topv, axis=-1)
        hidden = jax.nn.gelu(jnp.einsum('bld,efd->blef', x, w1) + b1, approximate=False)
        exp_out = jnp.einsum('blef,edf->bled', hidden, w2) + b2
        sel = jnp.take_along_axis(exp_out, topi[..., None], axis=2)
        fused = jnp.sum(w[..., None] * sel, axis=2)
        return fused

    def _L1_xattn_ref(x, context, ln_gamma, ln_beta, w_q, w_kv, w_out, b_out, gate):
        import jax, jax.numpy as jnp
        import numpy as np
        DIM = 128
        NUM_HEADS = 16
        DIM_HEAD = 64
        INNER = NUM_HEADS * DIM_HEAD
        SCALE = DIM_HEAD ** (-0.5)

        def _layernorm(x, gamma, beta, eps=1e-05):
            mu = jnp.mean(x, axis=-1, keepdims=True)
            var = jnp.mean(jnp.square(x - mu), axis=-1, keepdims=True)
            return (x - mu) * jax.lax.rsqrt(var + eps) * gamma + beta
        B, SQ, _ = x.shape
        SK = context.shape[1]
        xn = _layernorm(x, ln_gamma, ln_beta)
        q = (xn @ w_q).reshape(B, SQ, NUM_HEADS, DIM_HEAD)
        kv = context @ w_kv
        k, v = jnp.split(kv, 2, axis=-1)
        k = k.reshape(B, SK, NUM_HEADS, DIM_HEAD)
        v = v.reshape(B, SK, NUM_HEADS, DIM_HEAD)
        scores = jnp.einsum('bqhd,bkhd->bhqk', q * SCALE, k)
        attn = jax.nn.softmax(scores, axis=-1)
        out = jnp.einsum('bhqk,bkhd->bqhd', attn, v).reshape(B, SQ, INNER)
        out = out @ w_out + b_out
        return out * jnp.tanh(gate[0])

    def _L1_ffn_ref(x, gate_w, w1, w2):
        import jax, jax.numpy as jnp
        import numpy as np
        NUM_EXPERTS = 8
        EXPERT_CAPACITY = 2.0
        DIM = 128
        HIDDEN_DIM = 512
        n, t, d = x.shape
        e = gate_w.shape[0]
        k = int(EXPERT_CAPACITY * t / e)
        scores = jnp.einsum('ntd,ed->nte', x, gate_w)
        probs = jax.nn.softmax(scores, axis=-1)
        g, m = jax.lax.top_k(probs.transpose(0, 2, 1), k)
        batch_idx = jnp.arange(n)[:, None, None]
        xin = x[batch_idx, m]
        h = jnp.einsum('nekd,edf->nekf', xin, w1)
        h = jax.nn.gelu(h, approximate=False)
        h = jnp.einsum('nekf,efd->nekd', h, w2)
        out_tok = g[..., None] * h
        out = jnp.zeros((n, t, d), dtype=x.dtype).at[batch_idx, m].add(out_tok)
        return out

    def _L2_xattn_ref(x, knowledge_embeddings, Wq, bq, Wk, bk, Wv, bv, Wo, bo):
        import jax, jax.numpy as jnp
        import numpy as np
        import math
        D_MODEL = 128
        N_HEADS = 16
        HEAD_DIM = D_MODEL // N_HEADS
        TOP_K = 32
        SCALE = math.sqrt(HEAD_DIM)

        def _split_heads(t, n):
            B, L, _ = t.shape
            return t.reshape(B, L, N_HEADS, HEAD_DIM).transpose(0, 2, 1, 3)
        B, S, _ = x.shape
        N = knowledge_embeddings.shape[1]
        Q = _split_heads(x @ Wq.T + bq, N_HEADS)
        K = _split_heads(knowledge_embeddings @ Wk.T + bk, N_HEADS)
        V = _split_heads(knowledge_embeddings @ Wv.T + bv, N_HEADS)
        scores = jnp.einsum('bhsd,bhnd->bhsn', Q, K) / SCALE
        k = min(TOP_K, N)
        topk_scores, topk_indices = jax.lax.top_k(scores, k)
        sparse_weights = jax.nn.softmax(topk_scores, axis=-1)
        sel_V = jnp.take_along_axis(V[:, :, None, :, :], topk_indices[..., None], axis=3)
        context = jnp.einsum('bhsk,bhskd->bhsd', sparse_weights, sel_V)
        context = context.transpose(0, 2, 1, 3).reshape(B, S, D_MODEL)
        return context @ Wo.T + bo

    def _L2_ffn_ref(x, Wq, Wkv, Ws, Wo, bo):
        import jax, jax.numpy as jnp
        import numpy as np
        B, T, DIM, H, DH, TOPK = (4, 256, 128, 8, 64, 3)
        b, t, _ = x.shape
        s = jax.nn.sigmoid(x @ Ws)
        vals, idx = jax.lax.top_k(s, TOPK)
        bi = jnp.arange(b)[:, None, None]
        ti = jnp.arange(t)[None, :, None]
        scores = jnp.zeros_like(s).at[bi, ti, idx].set(vals)
        q = (x @ Wq).reshape(b, t, H, DH).transpose(0, 2, 1, 3)
        kv = (x @ Wkv).reshape(b, t, 2, H, DH).transpose(2, 0, 3, 1, 4)
        k, v = (kv[0], kv[1])
        scale = DH ** (-0.5)
        attn = jax.nn.softmax(jnp.einsum('bhid,bhjd->bhij', q * scale, k), axis=-1)
        out = jnp.einsum('bhij,bhjd->bhid', attn, v)
        proj = jnp.einsum('bhtd,hde->bhte', out, Wo) + bo[None, :, None, :]
        return jnp.einsum('bhte,bth->bte', proj, scores)

    def _L3_xattn_ref(x, context, Wq, Wk, Wv, Wo, bo):
        import jax, jax.numpy as jnp
        import numpy as np
        QUERY_DIM = 128
        CONTEXT_DIM = 128
        HEADS = 8
        DIM_HEAD = 64
        INNER = HEADS * DIM_HEAD
        SCALE = DIM_HEAD ** (-0.5)
        B, N, _ = x.shape
        M = context.shape[1]
        q = (x @ Wq).reshape(B, N, HEADS, DIM_HEAD)
        k = (context @ Wk).reshape(B, M, HEADS, DIM_HEAD)
        v = (context @ Wv).reshape(B, M, HEADS, DIM_HEAD)
        sim = jnp.einsum('bihd,bjhd->bhij', q.astype(jnp.float32), k.astype(jnp.float32)) * SCALE
        attn = jax.nn.softmax(sim, axis=-1).astype(v.dtype)
        out = jnp.einsum('bhij,bjhd->bihd', attn, v).reshape(B, N, INNER)
        return out @ Wo + bo

    def _L3_ffn_ref(x, W1, b1, W2, b2):
        import jax, jax.numpy as jnp
        import numpy as np
        EPS = 1e-05

        def _quantize(W):
            gamma = jnp.mean(jnp.abs(W))
            return jnp.clip(jnp.round(W / (gamma + EPS)), -1.0, 1.0)
        Wq1 = _quantize(W1)
        Wq2 = _quantize(W2)
        h = jax.nn.relu(jnp.einsum('bsd,fd->bsf', x, Wq1) + b1)
        out = jnp.einsum('bsf,df->bsd', h, Wq2) + b2
        return out
    x = x + _L0_xattn_ref(_layernorm(x, axis=-1), ctx_1024, ctx_1024, L0_xattn_Wq, L0_xattn_bq, L0_xattn_Wk, L0_xattn_bk, L0_xattn_Wv, L0_xattn_bv, L0_xattn_Wo, L0_xattn_bo)
    x = x + _L0_ffn_ref(_layernorm(x, axis=-1), L0_ffn_keys, L0_ffn_w1, L0_ffn_b1, L0_ffn_w2, L0_ffn_b2, L0_ffn_rw, L0_ffn_rb)
    x = x + _L1_xattn_ref(_layernorm(x, axis=-1), ctx_1024, L1_xattn_ln_gamma, L1_xattn_ln_beta, L1_xattn_w_q, L1_xattn_w_kv, L1_xattn_w_out, L1_xattn_b_out, L1_xattn_gate)
    x = x + _L1_ffn_ref(_layernorm(x, axis=-1), L1_ffn_gate_w, L1_ffn_w1, L1_ffn_w2)
    x = x + _L2_xattn_ref(_layernorm(x, axis=-1), ctx_1024, L2_xattn_Wq, L2_xattn_bq, L2_xattn_Wk, L2_xattn_bk, L2_xattn_Wv, L2_xattn_bv, L2_xattn_Wo, L2_xattn_bo)
    x = x + _L2_ffn_ref(_layernorm(x, axis=-1), L2_ffn_Wq, L2_ffn_Wkv, L2_ffn_Ws, L2_ffn_Wo, L2_ffn_bo)
    x = x + _L3_xattn_ref(_layernorm(x, axis=-1), ctx_1024, L3_xattn_Wq, L3_xattn_Wk, L3_xattn_Wv, L3_xattn_Wo, L3_xattn_bo)
    x = x + _L3_ffn_ref(_layernorm(x, axis=-1), L3_ffn_W1, L3_ffn_b1, L3_ffn_W2, L3_ffn_b2)
    return x

_drawn_inputs = setup_inputs


def setup_inputs(seed=0):
    import zlib

    import numpy as np

    out = dict(_drawn_inputs(seed))
    spreads = {'L0_xattn_bq': (0.0, 0.1),
     'L0_xattn_bk': (0.0, 2.0),
     'L0_xattn_bv': (0.0, 0.1),
     'L0_xattn_bo': (0.0, 0.1),
     'L0_ffn_b1': (0.0, 0.1),
     'L0_ffn_b2': (0.0, 0.1),
     'L0_ffn_rb': (0.0, 2.0),
     'L1_xattn_ln_gamma': (1.0, 0.2),
     'L1_xattn_ln_beta': (0.0, 0.1),
     'L1_xattn_b_out': (0.0, 0.1),
     'L2_xattn_bq': (0.0, 0.1),
     'L2_xattn_bk': (0.0, 2.0),
     'L2_xattn_bv': (0.0, 0.1),
     'L2_xattn_bo': (0.0, 0.1)}
    factors = {'L0_ffn_rw': 5.644,
     'L2_ffn_bo': 7.076,
     'L3_xattn_bo': 8.0,
     'L3_ffn_b1': 8.0,
     'L3_ffn_b2': 200.0}
    for name, (base, spread) in spreads.items():
        noise = np.random.default_rng([zlib.crc32(name.encode()), seed]).standard_normal(out[name].shape)
        drawn = base * np.exp(spread * noise) if base else spread * noise
        out[name] = jnp.asarray(drawn.astype(out[name].dtype))
    for name, factor in factors.items():
        out[name] = (out[name] * factor).astype(out[name].dtype)
    return out
```

```python
from contextlib import ExitStack

import concourse.bass as bass
from concourse import mybir

F32 = mybir.dt.float32
BF16 = mybir.dt.bfloat16
ALU = mybir.AluOpType
ACT = mybir.ActivationFunctionType
AX = mybir.AxisListType

P = 128
BATCH, SEQ, D = 4, 512, 128
TILES = SEQ // P
KEYS = 77
CTX = BATCH * KEYS
SLOTS = 2
H16, H8 = 16, 8
DH = 64
FT = 4
E0, E1 = 16, 8
TOP0, TOP1, TOP2, TOPF2 = 4, 128, 32, 3
EPS = 1e-5
TAKEN = -3.0e38
TAKEN_BELOW = -2.9e38
FILLER = 3.0e38
ROUND = 1.5 * 2.0 ** 23

VEC = {n: i for i, n in enumerate(
    ["bq0", "bk0", "bv0", "bo0", "bq2", "bk2", "bv2", "bo2", "gamma", "beta", "bo1", "bo3", "b2_3", "gate",
     "b1_3a", "b1_3b", "b1_3c", "b1_3d"])}
SMALL = {}
_at = 0
for _n, _w in (("vec", len(VEC)), ("ctxT", CTX), ("wq0", D), ("wk0", D), ("wv0", D), ("wo0", D), ("wq2", D),
               ("wk2", D), ("wv2", D), ("wo2", D), ("keysT", E0), ("rwT", E0), ("gwT", E1), ("wsT", H8),
               ("w1_3", FT * P), ("w2_3", FT * P)):
    SMALL[_n] = (_at, _w)
    _at += _w
SMALL_COLS = _at
EXPERT_COLS = 2 * FT * P + FT + 1
W_HEADS = 4


class Plan:

    def __init__(self):
        self.labels = {}
        self.per_turn = {}

    def start(self, sems):
        self.sems = sems

    def after(self, *label):
        engine, count = self.labels.get(label, ("pe", 0))
        return self.sems[engine], count

    def after_in(self, loop, i, *label, back=0):
        engine, count = self.labels.get(label, ("pe", 0))
        per = self.per_turn.get((engine, loop), 1)
        return self.sems[engine], i * per + max(0, count - back * per)


class Progress:
    def __init__(self, name, plan):
        self.name, self.plan, self.count = name, plan, 0

    def tick(self, *label):
        self.count += 1
        if label:
            self.plan.labels[label] = (self.name, self.count)
        return self.plan.sems[self.name], 1

    def now(self):
        return self.plan.sems[self.name], self.count

    def now_in(self, loop, i):
        return self.plan.sems[self.name], i * self.plan.per_turn.get((self.name, loop), 1) + self.count

    def loop_ends(self, loop, first, turns):
        per = self.count - first
        self.plan.per_turn[(self.name, loop)] = per
        self.count = first + turns * per


def network(nc, plan, x, small, heads1, heads3, headsF, experts0, experts1, rows, out):
    with ExitStack() as ctx:
        def sb(name, shape, dt=F32):
            return ctx.enter_context(nc.sbuf_tensor(name, shape, dt))

        def sem(name):
            return ctx.enter_context(nc.semaphore(name))

        sm = sb("small_weights", [P, SMALL_COLS])
        ident = sb("ident", [P, P])
        identb = sb("identb", [P, P], BF16)
        ones = sb("ones", [P, P])
        headmask = sb("headmask", [P, H16])
        sel = sb("sel", [P, E0, P], BF16)
        ctxk = {"X0": sb("kT0", [P, CTX]), "X2": sb("kT2", [P, CTX])}
        ctxv = {"X0": sb("vT0", [P, CTX]), "X2": sb("vT2", [P, CTX])}
        keys1 = sb("keys1", [P, BATCH, H16, KEYS])
        keys3 = sb("keys3", [P, BATCH, H8, KEYS])
        C = {"X0": sb("C0", [P, H16 * D]), "X1": sb("C1", [P, H16 * D]), "X2": sb("C2", [P, H16 * D]),
             "X3": sb("C3", [P, H8 * D])}
        AF = sb("AF", [P, H8 * D])
        CF = sb("CF", [P, H8 * D])
        W1q = sb("W1q", [P, FT * P])
        W2q = sb("W2q", [P, FT * P])
        R0 = sb("R0", [P, E0])
        c0row = sb("c0row", [1, E0])
        rbrow = sb("rbrow", [1, E0])
        boF = sb("boF", [H8, D])
        tg = sb("tanh_gate", [P, 1])
        bo1g = sb("bo1g", [P, 1])
        minus_half = sb("minus_half", [P, TILES])
        qsum = sb("qsum", [P, 2])
        qinv = sb("qinv", [P, 2])

        big = sb("big", [P, 2, H8 * SEQ])
        vp = sb("values", [P, 2, H16 * D])
        ee = sb("numerators", [P, 2, 2 * SEQ])
        kb = sb("keys", [P, 2, H16 * KEYS])
        wk = sb("topk_work", [P, 2, H8 * KEYS])
        we = sb("expert_weights", [P, 2, EXPERT_COLS])
        kpt = sb("keysF", [P, 2, SEQ])
        xs = sb("x_res", [P, SLOTS, TILES, D])
        xn = sb("xn", [P, SLOTS, TILES, D])
        xnT = sb("xnT", [P, SLOTS, SEQ])
        yT = sb("yT", [P, SLOTS, SEQ])
        cb = sb("gate_rows", [P, SLOTS, SEQ])
        qT = cb
        tmp = sb("gated", [P, SLOTS, SEQ])
        ctxb = sb("ctx_cols", [P, SLOTS, KEYS])
        stats = sb("stats", [P, SLOTS, TILES, 6])
        mv = sb("mv", [P, SLOTS, TILES, 2])
        ve = sb("ve", [P, SLOTS, TILES])
        rstd = sb("rstd", [P, SLOTS, TILES])
        mx = sb("mx", [P, 2, H8])
        sums = sb("sums", [P, 2, H8])
        rs = sb("rs", [P, 2, H8])
        m8a = sb("m8a", [P, 2, H8, 8])
        m8b = sb("m8b", [P, 2, H8, 8])
        sq = sb("sq", [P, SLOTS, TILES])
        lg = sb("lg", [P, SLOTS, TILES, E0 + 4])
        lgw = sb("lgw", [P, SLOTS, TILES, E0 + 4])
        m8r = sb("m8r", [P, SLOTS, TILES, 8])
        top = sb("top", [P, SLOTS, TILES, 8])
        ex = sb("ex", [P, SLOTS, TILES, E0])
        den = sb("den", [P, SLOTS, TILES])
        rden = sb("rden", [P, SLOTS, TILES])
        cw = sb("cw", [P, SLOTS, TILES, E0])
        c3 = sb("c3", [P, SLOTS, TILES, P], BF16)
        c3T = sb("c3T", [P, SLOTS, SEQ], BF16)
        prT = kpt[0:SLOTS * E1, 0, :]
        wkT = kpt[0:SLOTS * E1, 1, :]
        m16 = sb("m16", [SLOTS * E1, 8])
        pr = sb("pr", [P, TILES, SLOTS * E1])
        parts = wk[0:SLOTS * E1, 0:2, :].rearrange("p a b -> p (a b)")[:, 0:3 * SEQ // 2].bitcast(BF16)\
            .rearrange("p (k q) -> p k q", k=3)
        sg = sb("sg", [P, SLOTS, TILES, H8 + 5])
        sgw = sb("sgw", [P, SLOTS, TILES, H8 + 5])
        topF = sb("topF", [P, SLOTS, TILES, 8])
        gt = sb("gt", [P, SLOTS, TILES, H8])
        gtT = tmp[0:H8, :, :]
        dn = sb("dn", [P, 2, 2])
        rg = sb("rg", [P, 2, 2])

        sc = ctx.enter_context(nc.psum_tensor("scores", [P, 2, 2, SEQ], F32))
        tb = ctx.enter_context(nc.psum_tensor("turned", [P, 2, SEQ], F32))
        yb = ctx.enter_context(nc.psum_tensor("result", [P, SEQ], F32))
        mb = ctx.enter_context(nc.psum_tensor("misc", [P, SEQ], F32))

        sems = {n: sem(f"{n}_progress") for n in ("pe", "act", "dve", "pool")}
        x_in = [sem(f"x_in{s}") for s in range(SLOTS)]
        x_out = [sem(f"x_out{s}") for s in range(SLOTS)]
        w_in = [sem(f"expert_weights_in{j}") for j in range(2)]
        parts_in = sem("gate_parts_in")
        small_in = sem("small_in")
        rows_in = sem("rows_in")
        heads_in = [sem(f"heads{k}_in") for k in range(3)]
        every = list(sems.values()) + x_in + x_out + w_in + [parts_in, small_in, rows_in] + heads_in
        plan.start(sems)
        after, after_in = plan.after, plan.after_in

        def small_(name):
            a, w = SMALL[name]
            return sm[:, a:a + w]

        def vec(name, n=1):
            return sm[:, VEC[name]:VEC[name] + n]

        hp1 = [big[0:DH, k // 2, (k % 2) * 2048:(k % 2) * 2048 + 2048] for k in range(4)]
        hp3 = [vp[0:DH, k // 2, (k % 2) * 1024:(k % 2) * 1024 + 1024] for k in range(4)]
        hpF = [ee[0:DH, k, :] for k in range(2)] + [kb[0:DH, k, 0:1024] for k in range(2)]

        GROUPS = ([("A1", hp1, g) for g in range(4)] + [("C1", hp1, g) for g in range(4)]
                  + [("A3", hp3, g) for g in range(2)] + [("C3", hp3, g) for g in range(2)]
                  + [("AF", hpF, g) for g in range(2)] + [("CF", hpF, g) for g in range(2)])
        A1 = wk[:, :, :].rearrange("p a b -> p (a b)")
        with nc.Block() as block:
            @block.sync
            def _(sp):
                sp.dma_start(sm[:, :], small).then_inc(small_in, 16)
                for k in range(4):
                    sp.dma_start(hp1[k], heads1[k]).then_inc(heads_in[0], 16)

            @block.gpsimd
            def _(pool):
                g = Progress("pool", plan)
                nc.gpsimd.memset(ident[:, :], 0.0).then_inc(*g.tick())
                nc.gpsimd.memset(identb[:, :], 0.0).then_inc(*g.tick())
                nc.gpsimd.memset(headmask[:, :], 1.0).then_inc(*g.tick())
                nc.gpsimd.memset(sel[:, :, :], 0.0).then_inc(*g.tick())
                pool.wait_ge(*g.now())
                for m in (ident, identb):
                    nc.gpsimd.affine_select(out=m[:, :], in_=m[:, :], compare_op=ALU.not_equal, fill=1.0, base=0,
                                            pattern=[[-1, P]], channel_multiplier=1).then_inc(*g.tick("ident"))
                nc.gpsimd.affine_select(out=headmask[:, :], in_=headmask[:, :], compare_op=ALU.is_ge, fill=0.0,
                                        base=0, pattern=[[-8, H16]], channel_multiplier=1).then_inc(*g.tick())
                pool.wait_ge(*g.now())
                nc.gpsimd.affine_select(out=headmask[:, :], in_=headmask[:, :], compare_op=ALU.is_ge, fill=0.0,
                                        base=7, pattern=[[8, H16]], channel_multiplier=-1)\
                    .then_inc(*g.tick("headmask"))
                for k in range(3):
                    nc.gpsimd.affine_select(out=sel[:, :, :], in_=sel[:, :, :], compare_op=ALU.not_equal, fill=1.0,
                                            base=-E0 * k, pattern=[[-1, E0], [0, P]], channel_multiplier=1)\
                        .then_inc(*g.tick())
                    pool.wait_ge(*g.now())
                for k in range(4):
                    pool.dma_start(hpF[k], headsF[k]).then_inc(heads_in[2], 16)
                pool.wait_ge(small_in, 16)
                for st, w in (("X0", "wo0"), ("X2", "wo2")):
                    nc.gpsimd.tensor_tensor(
                        C[st][:, :].rearrange("p (h e) -> p h e", h=H16),
                        small_(w).unsqueeze(1).to_broadcast([P, H16, D]),
                        headmask[:, :].unsqueeze(2).to_broadcast([P, H16, D]), ALU.mult).then_inc(*g.tick())
                pool.wait_ge(*g.now())
                pool.wait_ge(*g.now())

            @block.scalar
            def _(act):
                a = Progress("act", plan)
                act.dma_start(rbrow[:, :], rows[0:1, 0:E0]).then_inc(rows_in, 16)
                act.dma_start(boF[:, :], rows[1:1 + H8, :]).then_inc(rows_in, 16)
                for k in range(4):
                    act.dma_start(hp3[k], heads3[k]).then_inc(heads_in[1], 16)
                act.wait_ge(small_in, 16)
                nc.scalar.activation(tg[:, :], vec("gate"), ACT.Tanh).then_inc(*a.tick("tanh"))
                for n, (dst, b) in enumerate(((ctxk["X0"], "bk0"), (ctxv["X0"], "bv0"),
                                              (ctxk["X2"], "bk2"), (ctxv["X2"], "bv2"))):
                    act.wait_ge(*after("pro ctx", n))
                    nc.scalar.activation(dst[:, :], sc[:, n // 2, n % 2, 0:CTX], ACT.Identity, bias=vec(b))\
                        .then_inc(*a.tick("pro ctx out", n))
                for n, (kind, _, grp) in enumerate(GROUPS):
                    act.wait_ge(*after("pro group", n))
                    if kind in ("A1", "A3"):
                        if n >= 2:
                            act.wait_ge(*after("pro group used", max(0, n - 2)))
                        act_dst = A1[:, (n % 2) * 512:(n % 2) * 512 + 512]
                    else:
                        act_dst = {"C1": C["X1"], "C3": C["X3"], "AF": AF, "CF": CF}[kind][:, grp * 512:grp * 512 + 512]
                    scale = DH ** -0.5 if kind == "AF" else 1.0
                    nc.scalar.activation(act_dst, tb[:, n % 2, :], ACT.Copy, scale=scale)\
                        .then_inc(*a.tick("pro group out", n))
                act.wait_ge(*a.now())

            @block.vector
            def _(dve):
                v = Progress("dve", plan)
                nc.vector.memset(ones[:, :], 1.0).then_inc(*v.tick("ones"))
                nc.vector.memset(minus_half[:, :], -0.5).then_inc(*v.tick())
                nc.vector.memset(c3[:, :, :, :], 0.0).then_inc(*v.tick())
                nc.vector.memset(c3T[:, :, :], 0.0).then_inc(*v.tick())
                nc.vector.memset(top[:, :, :, :], FILLER).then_inc(*v.tick())
                nc.vector.memset(topF[:, :, :, :], FILLER).then_inc(*v.tick())
                nc.vector.memset(lg[:, :, :, :], FILLER).then_inc(*v.tick())
                nc.vector.memset(sg[:, :, :, :], FILLER).then_inc(*v.tick())
                dve.wait_ge(small_in, 16)
                nc.vector.scalar_tensor_tensor(R0[:, :], small_("keysT"), 2.0, small_("rwT"), ALU.mult, ALU.add)\
                    .then_inc(*v.tick())
                nc.vector.tensor_tensor(lgw[:, 0, 0, 0:E0], small_("keysT"), small_("keysT"), ALU.mult)\
                    .then_inc(*v.tick("key squares"))
                dve.wait_ge(*after("key norms"))
                dve.wait_ge(rows_in, 32)
                nc.vector.tensor_tensor(c0row[:, :], rbrow[:, :], mb[0:1, 0:E0], ALU.subtract).then_inc(*v.tick())
                dve.wait_ge(*after("tanh"))
                nc.vector.tensor_tensor(bo1g[:, :], vec("bo1"), tg[:, :], ALU.mult).then_inc(*v.tick())
                for k, w in enumerate(("w1_3", "w2_3")):
                    nc.vector.tensor_reduce(qsum[:, k:k + 1], small_(w), AX.X, ALU.add, apply_absolute_value=True)\
                        .then_inc(*v.tick("abs sums"))
                dve.wait_ge(*after("abs means"))
                nc.vector.tensor_scalar(qinv[:, :], yb[:, 0:2], 1.0 / (D * FT * P), EPS, ALU.mult, ALU.add)\
                    .then_inc(*v.tick())
                dve.wait_ge(*v.now())
                nc.vector.reciprocal(qinv[:, :], qinv[:, :]).then_inc(*v.tick())
                dve.wait_ge(*v.now())
                for k, (w, dst) in enumerate((("w1_3", W1q), ("w2_3", W2q))):
                    nc.vector.tensor_scalar(dst[:, :], small_(w), qinv[:, k:k + 1], 1.0, ALU.mult, ALU.min)\
                        .then_inc(*v.tick())
                    dve.wait_ge(*v.now())
                    nc.vector.tensor_scalar(dst[:, :], dst[:, :], -1.0, ROUND, ALU.max, ALU.add).then_inc(*v.tick())
                    dve.wait_ge(*v.now())
                    nc.vector.tensor_scalar(dst[:, :], dst[:, :], -ROUND, None, ALU.add).then_inc(*v.tick())
                for n in [n for n, g in enumerate(GROUPS) if g[0] in ("A1", "A3")]:
                    kind, _, grp = GROUPS[n]
                    for i in range(4):
                        dve.wait_ge(*after("pro keys", n, i))
                        dst = keys1 if kind == "A1" else keys3
                        nc.vector.tensor_copy(
                            dst[:, :, 4 * grp + i, :],
                            sc[:, i // 2, i % 2, 0:CTX].rearrange("p (b k) -> p b k", b=BATCH))\
                            .then_inc(*v.tick("pro keys out", n, i))
                dve.wait_ge(*v.now())

            @block.tensor
            def _(pe):
                t = Progress("pe", plan)
                pe.wait_ge(small_in, 16)
                for n, w in enumerate(("wk0", "wv0", "wk2", "wv2")):
                    nc.tensor.matmul(sc[:, n // 2, n % 2, 0:CTX], small_(w), small_("ctxT"), start=True, stop=True)\
                        .then_inc(*t.tick("pro ctx", n))
                pe.wait_ge(*after("key squares"))
                nc.tensor.matmul(mb[0:1, 0:E0], ones[:, 0:1], lgw[:, 0, 0, 0:E0], start=True, stop=True)\
                    .then_inc(*t.tick("key norms"))
                pe.wait_ge(*after("abs sums"))
                nc.tensor.matmul(yb[:, 0:2], ones[:, :], qsum[:, :], start=True, stop=True)\
                    .then_inc(*t.tick("abs means"))
                pe.wait_ge(heads_in[0], 64)
                pe.wait_ge(heads_in[1], 64)
                pe.wait_ge(heads_in[2], 64)

                def keys_of(n):
                    pe.wait_ge(*after("pro group out", n))
                    for i in range(4):
                        if keys_of.last is None:
                            pe.wait_ge(*after("pro ctx out", i))
                        else:
                            pe.wait_ge(*after("pro keys out", keys_of.last, i))
                        ins = nc.tensor.matmul(sc[:, i // 2, i % 2, 0:CTX],
                                               A1[:, (n % 2) * 512 + i * P:(n % 2) * 512 + i * P + P],
                                               small_("ctxT"), start=True, stop=True)
                        ins.then_inc(*t.tick("pro keys", n, i))
                    plan.labels[("pro group used", n)] = ("pe", t.count)
                    keys_of.last = n

                keys_of.last = None
                pending = None
                for n, (kind, hp, grp) in enumerate(GROUPS):
                    if n >= 2:
                        pe.wait_ge(*after("pro group out", n - 2))
                    first, second = (1, 0) if kind[0] == "A" else (2, 3)
                    for i in range(4):
                        h = 4 * grp + i
                        ins = nc.tensor.matmul(tb[:, n % 2, i * P:(i + 1) * P], hp[first][:, h * P:(h + 1) * P],
                                               hp[second][:, h * P:(h + 1) * P], start=True, stop=True)
                    ins.then_inc(*t.tick("pro group", n))
                    if pending is not None:
                        keys_of(pending)
                    pending = n if kind in ("A1", "A3") else None
                pe.wait_ge(*t.now())

        ATT = {"X0": H16, "X1": H16, "X2": H16, "X3": H8}
        HEADROWS = {"X0", "X2"}
        SCALE = {"X0": 8 ** -0.5, "X1": DH ** -0.5, "X2": 8 ** -0.5, "X3": DH ** -0.5}
        STAGES = [("X0", 0), ("X0", 1), ("F0", None), ("X1", 0), ("X1", 1), ("F1", None),
                  ("X2", 0), ("X2", 1), ("F2", 0), ("F2", 1), ("X3", 0), ("X3", 1), ("F3", 0), ("F3", 1)]
        slots_of = lambda s: range(SLOTS) if s is None else (s,)
        EXPERTS = {"F0": E0, "F1": E1}

        def big_slot(st, s, hf):
            return s if st == "X3" else hf


        with nc.Fori(0, BATCH // SLOTS) as turn:
            with nc.Block() as block:
                @block.sync
                def _(sp):
                    for q in every:
                        sp.sem_clear(q)

            with nc.Block() as block:
                @block.sync
                def _(sp):
                    for s in range(SLOTS):
                        sp.dma_start(xs[:, s], x[turn * SLOTS + s].rearrange("(t p) d -> p t d", p=P))\
                            .then_inc(x_in[s], 16)
                    for st, packs in (("F0", experts0), ("F1", experts1)):
                        if st == "F1":
                            sp.wait_ge(*after("parts", st))
                            for k in range(3):
                                for s in range(SLOTS):
                                    sp.dma_start(c3T[SLOTS * E1 * k:SLOTS * E1 * (k + 1), s], parts[:, k, :])\
                                        .then_inc(parts_in, 16)
                        with sp.Fori(0, EXPERTS[st] // 2) as i:
                            for j in range(2):
                                sp.wait_ge(*after_in(st, i, "gated", st, j, 1, back=1))
                                sp.dma_start(we[:, j, :], packs[2 * i + j]).then_inc(w_in[j], 16)
                    for s in range(SLOTS):
                        sp.wait_ge(*after("x done", "F3", s))
                        sp.dma_start(out[turn * SLOTS + s].rearrange("(t p) d -> p t d", p=P), xs[:, s])\
                            .then_inc(x_out[s], 16)
                    for s in range(SLOTS):
                        sp.wait_ge(x_out[s], 16)

                @block.tensor
                def _(pe):
                    t = Progress("pe", plan)
                    last = {}

                    def claim(bank, key):
                        if bank in last:
                            pe.wait_ge(*after("read", bank, *last[bank]))
                        last[bank] = key

                    def turned(st, s):
                        claim("tb0", (st, s, "xn"))
                        pe.wait_ge(*after("xn", st, s))
                        for k in range(TILES):
                            ins = nc.tensor.transpose(tb[:, 0, k * P:(k + 1) * P], xn[:, s, k, :], ident[:, :])
                        ins.then_inc(*t.tick("tb0", st, s, "xn"))

                    def turned_back(st, s):
                        claim("tb0", (st, s, "y"))
                        pe.wait_ge(*after("yT", st, s))
                        for k in range(TILES):
                            ins = nc.tensor.transpose(tb[:, 0, k * P:(k + 1) * P], yT[:, s, k * P:(k + 1) * P],
                                                      ident[:, :])
                        ins.then_inc(*t.tick("tb0", st, s, "y"))

                    def attention(st, s):
                        heads = ATT[st]
                        halves = heads // H8
                        turned(st, s)
                        pe.wait_ge(*after("xnT", st, s))
                        if st in HEADROWS:
                            claim("yb", (st, s, "q"))
                            nc.tensor.matmul(yb[:, :], small_("wq0" if st == "X0" else "wq2"), xnT[:, s, :],
                                             start=True, stop=True).then_inc(*t.tick("yb", st, s, "q"))
                        pe.wait_ge(*after("ctx cols", st, s))
                        for n in range(heads // 4):
                            claim("mb", (st, s, "v", n))
                            nc.tensor.matmul(mb[0:KEYS, :], ctxb[:, s, :], C[st][:, n * 512:(n + 1) * 512],
                                             start=True, stop=True).then_inc(*t.tick("mb", st, s, "v", n))
                        query = qT if st in HEADROWS else xnT
                        if st in HEADROWS:
                            pe.wait_ge(*after("qT", st, s))
                        pe.wait_ge(*after("keys", st, s))

                        def scores(u):
                            hf, k, p = u // TILES, u % TILES, u % 2
                            claim(f"sc{p}", (st, s, u))
                            for j in range(2):
                                c = (hf * H8 + 4 * j) * KEYS
                                ins = nc.tensor.matmul(sc[:, p, j, 0:4 * KEYS], query[:, s, k * P:(k + 1) * P],
                                                       kb[:, s, c:c + 4 * KEYS], start=True, stop=True)
                            ins.then_inc(*t.tick(f"sc{p}", st, s, u))

                        def turn_probs(u):
                            p = u % 2
                            pe.wait_ge(*after("probs", st, s, u))
                            for j in range(2):
                                claim(f"tb{j}", (st, s, u))
                                for i in range(4):
                                    ins = nc.tensor.transpose(tb[0:KEYS, j, i * P:(i + 1) * P],
                                                              ee[:, p, (4 * j + i) * KEYS:(4 * j + i + 1) * KEYS],
                                                              ident[:, :])
                                ins.then_inc(*t.tick(f"tb{j}", st, s, u))

                        def values(hf):
                            if hf == 0:
                                claim("yb", (st, s, "y"))
                            for n in range(heads // 4):
                                pe.wait_ge(*after("read", "mb", st, s, "v", n))
                            for j in range(2):
                                pe.wait_ge(*after("read", f"tb{j}", st, s, hf * TILES + TILES - 1))
                            slot = big_slot(st, s, hf)
                            for h in range(H8):
                                g = hf * H8 + h
                                ins = nc.tensor.matmul(yb[:, :], vp[0:KEYS, s, g * D:(g + 1) * D],
                                                       big[0:KEYS, slot, h * SEQ:(h + 1) * SEQ],
                                                       start=(g == 0), stop=(g == heads - 1))
                            ins.then_inc(*t.tick("values", st, s, hf))
                            if hf == halves - 1:
                                plan.labels[("yb", st, s, "y")] = ("pe", t.count)

                        units = halves * TILES
                        scores(0)
                        scores(1)
                        for u in range(units):
                            turn_probs(u)
                            if u + 2 < units:
                                scores(u + 2)
                            if u == TILES + 1:
                                values(0)
                        values(halves - 1)
                        turned_back(st, s)

                    def experts(st):
                        for s in range(SLOTS):
                            turned(st, s)
                            pe.wait_ge(*after("xnT", st, s))
                            claim("mb", (st, s, "logits"))
                            for k in range(TILES):
                                tile = xnT[:, s, k * P:(k + 1) * P]
                                if st == "F0":
                                    nc.tensor.matmul(mb[:, k * E0:(k + 1) * E0], tile, R0[:, :],
                                                     start=True, stop=False)
                                    ins = nc.tensor.matmul(mb[:, k * E0:(k + 1) * E0], ones[0:1, :], c0row[:, :],
                                                           start=False, stop=True)
                                else:
                                    ins = nc.tensor.matmul(mb[:, k * E1:(k + 1) * E1], tile, small_("gwT"),
                                                           start=True, stop=True)
                            ins.then_inc(*t.tick("mb", st, s, "logits"))
                        if st == "F0":
                            mbb = mb[:, :].bitcast(BF16)
                            for s in range(SLOTS):
                                claim("mb", (st, s, "gates"))
                                pe.wait_ge(*after("gate parts", st, s))
                                for k in range(TILES):
                                    ins = nc.tensor.transpose(mbb[:, k * P:(k + 1) * P], c3[:, s, k, :], identb[:, :])
                                ins.then_inc(*t.tick("mb", st, s, "gates"))
                        else:
                            claim("mb", (st, "probs"))
                            pe.wait_ge(*after("expert probs", st))
                            for k in range(TILES):
                                ins = nc.tensor.transpose(mb[0:SLOTS * E1, k * P:(k + 1) * P], pr[:, k, :], ident[:, :])
                            ins.then_inc(*t.tick("mb", st, "probs"))
                        for bank in ("sc0", "sc1", "tb0", "tb1", "mb"):
                            claim(bank, (st, "loop", bank))
                        if st == "F0":
                            for s in range(SLOTS):
                                pe.wait_ge(*after("read", "mb", st, s, "gates"))
                        else:
                            pe.wait_ge(parts_in, 16 * 3 * SLOTS)
                        first = t.count
                        loads = 0 if st == "F0" else E0 // 2
                        with pe.Fori(0, EXPERTS[st] // 2) as i:
                            for j in range(2):
                                pe.wait_ge(w_in[j], i * 16 + 16 * (loads + 1))
                                for s in range(SLOTS):
                                    n = SLOTS * j + s
                                    for q in range(2):
                                        if n:
                                            pe.wait_ge(*after_in(st, i, "hidden", st, n - 1, q))
                                        else:
                                            pe.wait_ge(*after_in(st, i, "hidden", st, 2 * SLOTS - 1, q, back=1))
                                        for h in range(2):
                                            f = 2 * q + h
                                            ins = nc.tensor.matmul(sc[:, q, h, :], we[:, j, f * P:(f + 1) * P],
                                                                   xnT[:, s, :], start=True, stop=True)
                                        ins.then_inc(*t.tick("hidden in", st, n, q))
                                    if n:
                                        pe.wait_ge(*after_in(st, i, "gate row", st, n - 1))
                                    else:
                                        pe.wait_ge(*after_in(st, i, "gate row", st, 2 * SLOTS - 1, back=1))
                                    row = 2 * i + j + (0 if st == "F0" else s * E1)
                                    nc.tensor.matmul(mb[:, :], sel[:, row, :], c3T[:, s, :], start=True, stop=True)\
                                        .then_inc(*t.tick("gate row in", st, n))
                                    if n >= SLOTS:
                                        pe.wait_ge(*after_in(st, i, "gated", st, j - 1, s))
                                    else:
                                        pe.wait_ge(*after_in(st, i, "gated", st, 1, s, back=1))
                                    for f in range(FT):
                                        if f % 2 == 0:
                                            pe.wait_ge(*after_in(st, i, "hidden", st, n, f // 2))
                                        ins = nc.tensor.matmul(tb[:, s, :], we[:, j, (FT + f) * P:(FT + f + 1) * P],
                                                               big[:, s, f * SEQ:(f + 1) * SEQ],
                                                               start=(f == 0), stop=(f == FT - 1))
                                    ins.then_inc(*t.tick("expert out", st, n))
                        t.loop_ends(st, first, EXPERTS[st] // 2)
                        for s in range(SLOTS):
                            turned_back(st, s)

                    def self_attention(st, s):
                        turned(st, s)
                        pe.wait_ge(*after("xnT", st, s))
                        claim("mb", (st, s, "gate"))
                        for k in range(TILES):
                            ins = nc.tensor.matmul(mb[:, k * H8:(k + 1) * H8], xnT[:, s, k * P:(k + 1) * P],
                                                   small_("wsT"), start=True, stop=True)
                        ins.then_inc(*t.tick("mb", st, s, "gate"))

                        def value_group(g):
                            for k in range(TILES):
                                claim("mb", (st, s, "v", g, k))
                                nc.tensor.matmul(mb[:, :], xnT[:, s, k * P:(k + 1) * P], CF[:, g * 512:(g + 1) * 512],
                                                 start=True, stop=True).then_inc(*t.tick("mb", st, s, "v", g, k))

                        def keys(h):
                            claim("mb", (st, s, "k", h))
                            nc.tensor.matmul(mb[:, :], AF[:, h * P:(h + 1) * P], xnT[:, s, :], start=True, stop=True)\
                                .then_inc(*t.tick("mb", st, s, "k", h))

                        def scores(h, r):
                            claim(f"sc{r}", (st, s, h))
                            if r == 0:
                                pe.wait_ge(*after("read", "mb", st, s, "k", h))
                            for i in range(2):
                                k = 2 * r + i
                                ins = nc.tensor.matmul(sc[:, r, i, :], xnT[:, s, k * P:(k + 1) * P], kpt[:, h % 2, :],
                                                       start=True, stop=True)
                            ins.then_inc(*t.tick(f"sc{r}", st, s, h))

                        def turn_probs(h, r):
                            pe.wait_ge(*after("probs", st, s, h, r))
                            for i in range(2):
                                claim(f"tb{i}", (st, s, h, r))
                                for k in range(TILES):
                                    ins = nc.tensor.transpose(tb[:, i, k * P:(k + 1) * P],
                                                              ee[:, r, i * SEQ + k * P:i * SEQ + (k + 1) * P],
                                                              ident[:, :])
                                ins.then_inc(*t.tick(f"tb{i}", st, s, h, r))

                        def values(h):
                            for i in range(2):
                                pe.wait_ge(*after("read", f"tb{i}", st, s, h, 1))
                            for k in range(TILES):
                                c = k * 512 + (h % 4) * D
                                ins = nc.tensor.matmul(yb[:, :], vp[:, h // 4, c:c + D],
                                                       big[:, h % 2, k * SEQ:(k + 1) * SEQ], start=False,
                                                       stop=(h == H8 - 1 and k == TILES - 1))
                            ins.then_inc(*t.tick("values", st, s, h))
                            if h == H8 - 1:
                                plan.labels[("yb", st, s, "y")] = ("pe", t.count)

                        keys(0)
                        scores(0, 0)
                        scores(0, 1)
                        value_group(0)
                        claim("mb", (st, s, "gatesT"))
                        pe.wait_ge(*after("gates", st, s))
                        for k in range(TILES):
                            ins = nc.tensor.transpose(mb[0:H8, k * P:(k + 1) * P], gt[:, s, k, :], ident[:, :])
                        ins.then_inc(*t.tick("mb", st, s, "gatesT"))
                        claim("yb", (st, s, "y"))
                        pe.wait_ge(*after("read", "mb", st, s, "gatesT"))
                        nc.tensor.matmul(yb[:, :], boF[:, :], gtT[:, s, :], start=True, stop=False)
                        for h in range(H8):
                            if h + 1 < H8:
                                keys(h + 1)
                            for r in range(2):
                                turn_probs(h, r)
                                if h + 1 < H8:
                                    scores(h + 1, r)
                            if h == 1:
                                value_group(1)
                            if h >= 1:
                                values(h - 1)
                        values(H8 - 1)
                        turned_back(st, s)

                    def ternary(st, s):
                        turned(st, s)
                        pe.wait_ge(*after("xnT", st, s))
                        for q in range(2):
                            claim(f"sc{q}", (st, s))
                            for h in range(2):
                                f = 2 * q + h
                                ins = nc.tensor.matmul(sc[:, q, h, :], W1q[:, f * P:(f + 1) * P], xnT[:, s, :],
                                                       start=True, stop=True)
                            ins.then_inc(*t.tick(f"sc{q}", st, s))
                        claim("yb", (st, s, "y"))
                        for f in range(FT):
                            if f % 2 == 0:
                                pe.wait_ge(*after("read", f"sc{f // 2}", st, s))
                            ins = nc.tensor.matmul(yb[:, :], W2q[:, f * P:(f + 1) * P],
                                                   big[:, s, f * SEQ:(f + 1) * SEQ], start=(f == 0), stop=(f == FT - 1))
                        ins.then_inc(*t.tick("yb", st, s, "y"))
                        turned_back(st, s)

                    for st, s in STAGES:
                        if st in ATT:
                            attention(st, s)
                        elif st in EXPERTS:
                            experts(st)
                        elif st == "F2":
                            self_attention(st, s)
                        else:
                            ternary(st, s)
                    pe.wait_ge(*t.now())

                @block.scalar
                def _(act):
                    a = Progress("act", plan)

                    def turned(st, s):
                        act.wait_ge(*after("tb0", st, s, "xn"))
                        if st == "X1":
                            nc.scalar.activation(xnT[:, s, :], tb[:, 0, :], ACT.Identity, bias=vec("beta"),
                                                 scale=vec("gamma")).then_inc(*a.tick("xnT", st, s))
                        else:
                            nc.scalar.activation(xnT[:, s, :], tb[:, 0, :], ACT.Copy).then_inc(*a.tick("xnT", st, s))
                        plan.labels[("read", "tb0", st, s, "xn")] = ("act", a.count)

                    def result(st, s):
                        act.wait_ge(*after("yb", st, s, "y"))
                        if st == "X1":
                            ins = nc.scalar.activation(yT[:, s, :], yb[:, :], ACT.Identity, bias=bo1g[:, :],
                                                       scale=tg[:, :])
                        elif st == "F2":
                            ins = nc.scalar.activation(yT[:, s, :], yb[:, :], ACT.Copy)
                        else:
                            b = {"X0": "bo0", "X2": "bo2", "X3": "bo3", "F3": "b2_3"}[st]
                            ins = nc.scalar.activation(yT[:, s, :], yb[:, :], ACT.Identity, bias=vec(b))
                        ins.then_inc(*a.tick("yT", st, s))
                        plan.labels[("read", "yb", st, s, "y")] = ("act", a.count)

                    def attention(st, s):
                        heads = ATT[st]
                        turned(st, s)
                        if st in HEADROWS:
                            act.wait_ge(*after("yb", st, s, "q"))
                            nc.scalar.activation(qT[:, s, :], yb[:, :], ACT.Identity,
                                                 bias=vec("bq0" if st == "X0" else "bq2"))\
                                .then_inc(*a.tick("qT", st, s))
                            plan.labels[("read", "yb", st, s, "q")] = ("act", a.count)
                        for n in range(heads // 4):
                            act.wait_ge(*after("mb", st, s, "v", n))
                            nc.scalar.activation(vp[0:KEYS, s, n * 512:(n + 1) * 512], mb[0:KEYS, :], ACT.Copy)\
                                .then_inc(*a.tick("read", "mb", st, s, "v", n))

                        def exps(u):
                            act.wait_ge(*after("shifted", st, s, u))
                            nc.scalar.activation(ee[:, u % 2, 0:H8 * KEYS], ee[:, u % 2, 0:H8 * KEYS], ACT.Exp,
                                                 scale=SCALE[st]).then_inc(*a.tick("exps", st, s, u))

                        def store(u):
                            hf, k = u // TILES, u % TILES
                            slot = big_slot(st, s, hf)
                            if u % TILES == 0:
                                wait_big(slot)
                            dst = big[:, slot, :].rearrange("p (h q) -> p h q", h=H8)
                            for j in range(2):
                                act.wait_ge(*after(f"tb{j}", st, s, u))
                                nc.scalar.activation(dst[0:KEYS, 4 * j:4 * j + 4, k * P:(k + 1) * P],
                                                     tb[0:KEYS, j, :].rearrange("p (h q) -> p h q", h=4), ACT.Copy)\
                                    .then_inc(*a.tick("read", f"tb{j}", st, s, u))
                            if k == TILES - 1:
                                big_user[slot] = ("values", st, s, hf)

                        units = heads // H8 * TILES
                        exps(0)
                        for u in range(units):
                            if u + 1 < units:
                                exps(u + 1)
                            store(u)
                        result(st, s)

                    big_user = {}

                    def wait_big(slot):
                        if slot in big_user:
                            act.wait_ge(*after(*big_user[slot]))

                    def experts(st):
                        if st == "F0":
                            for s in range(SLOTS):
                                act.wait_ge(*after("xn", st, s))
                                for k in range(TILES):
                                    nc.scalar.activation(tmp[:, s, k * D:(k + 1) * D], xn[:, s, k, :], ACT.Square,
                                                         accum_out=sq[:, s, k:k + 1]).then_inc(*a.tick("norms", st, s))
                        for s in range(SLOTS):
                            turned(st, s)
                        for s in range(SLOTS):
                            act.wait_ge(*after("router shifted", st, s))
                            n = E0 if st == "F0" else E1
                            nc.scalar.activation(ex[:, s, :, 0:n], ex[:, s, :, 0:n], ACT.Exp)\
                                .then_inc(*a.tick("router exps", st, s))
                        if st == "F0":
                            mbb = mb[:, :].bitcast(BF16)
                            for s in range(SLOTS):
                                act.wait_ge(*after("mb", st, s, "gates"))
                                nc.scalar.activation(c3T[:, s, :], mbb[:, 0:SEQ], ACT.Copy)\
                                    .then_inc(*a.tick("read", "mb", st, s, "gates"))
                        else:
                            act.wait_ge(*after("mb", st, "probs"))
                            nc.scalar.activation(prT[:, :], mb[0:SLOTS * E1, :], ACT.Copy)\
                                .then_inc(*a.tick("read", "mb", st, "probs"))
                        for s in range(SLOTS):
                            wait_big(s)
                        first = a.count
                        with act.Fori(0, EXPERTS[st] // 2) as i:
                            for j in range(2):
                                for s in range(SLOTS):
                                    n = SLOTS * j + s
                                    b1 = we[:, j, 2 * FT * P:2 * FT * P + FT]
                                    for q in range(2):
                                        act.wait_ge(*after_in(st, i, "hidden in", st, n, q))
                                        if st == "F0":
                                            for h in range(2):
                                                f = 2 * q + h
                                                ins = nc.scalar.activation(big[:, s, f * SEQ:(f + 1) * SEQ],
                                                                           sc[:, q, h, :], ACT.Gelu,
                                                                           bias=b1[:, f:f + 1])
                                        else:
                                            ins = nc.scalar.activation(big[:, s, 2 * q * SEQ:2 * (q + 1) * SEQ],
                                                                       sc[:, q, :, :].rearrange("p a b -> p (a b)"),
                                                                       ACT.Gelu)
                                        ins.then_inc(*a.tick("hidden", st, n, q))
                                    act.wait_ge(*after_in(st, i, "gate row in", st, n))
                                    if n >= SLOTS:
                                        act.wait_ge(*after_in(st, i, "gated", st, j - 1, s))
                                    else:
                                        act.wait_ge(*after_in(st, i, "gated", st, 1, s, back=1))
                                    nc.scalar.activation(cb[:, s, :], mb[:, :], ACT.Copy)\
                                        .then_inc(*a.tick("gate row", st, n))
                        a.loop_ends(st, first, EXPERTS[st] // 2)
                        for q in range(2):
                            plan.labels[("read", f"sc{q}", st, "loop", f"sc{q}")] = ("act", a.count)
                        plan.labels[("read", "mb", st, "loop", "mb")] = ("act", a.count)
                        for s in range(SLOTS):
                            big_user[s] = ("tb0", st, SLOTS - 1, "y")

                    def self_attention(st, s):
                        turned(st, s)
                        act.wait_ge(*after("mb", st, s, "gate"))
                        nc.scalar.activation(sg[:, s, :, 0:H8], mb[:, 0:TILES * H8].rearrange("p (t h) -> p t h", h=H8),
                                             ACT.Exp, scale=-1.0).then_inc(*a.tick("read", "mb", st, s, "gate"))

                        def keys(h):
                            act.wait_ge(*after("mb", st, s, "k", h))
                            if h >= 2:
                                act.wait_ge(*after("sc1", st, s, h - 2))
                            nc.scalar.activation(kpt[:, h % 2, :], mb[:, :], ACT.Copy)\
                                .then_inc(*a.tick("read", "mb", st, s, "k", h))

                        def value_group(g):
                            for k in range(TILES):
                                act.wait_ge(*after("mb", st, s, "v", g, k))
                                nc.scalar.activation(vp[:, g, k * 512:(k + 1) * 512], mb[:, :], ACT.Copy)\
                                    .then_inc(*a.tick("read", "mb", st, s, "v", g, k))

                        def exps(h, r):
                            act.wait_ge(*after("maxima", st, s, h, r))
                            if (h, r) != (0, 0) and h:
                                act.wait_ge(*after("tb1", st, s, h - 1, r))
                            for i in range(2):
                                nc.scalar.activation(ee[:, r, i * SEQ:(i + 1) * SEQ], sc[:, r, i, :], ACT.Exp,
                                                     bias=mx[:, r, i:i + 1], accum_out=dn[:, r, i:i + 1])\
                                    .then_inc(*a.tick("exps", st, s, h, r))
                            plan.labels[("read", f"sc{r}", st, s, h)] = ("act", a.count)

                        def store(h, r):
                            if r == 0:
                                wait_big(h % 2)
                            dst = big[:, h % 2, 0:TILES * SEQ].rearrange("p (k q) -> p k q", k=TILES)
                            act.wait_ge(*after("tb0", st, s, h, r))
                            nc.scalar.activation(dst[:, :, 2 * r * P:(2 * r + 1) * P],
                                                 tb[:, 0, :].rearrange("p (k q) -> p k q", k=TILES), ACT.Copy)\
                                .then_inc(*a.tick("read", "tb0", st, s, h, r))
                            if r == 1:
                                big_user[h % 2] = ("values", st, s, h)

                        keys(0)
                        exps(0, 0)
                        exps(0, 1)
                        value_group(0)
                        act.wait_ge(*after("mb", st, s, "gatesT"))
                        nc.scalar.activation(gtT[:, s, :], mb[0:H8, :], ACT.Copy)\
                            .then_inc(*a.tick("read", "mb", st, s, "gatesT"))
                        for h in range(H8):
                            if h + 1 < H8:
                                keys(h + 1)
                            for r in range(2):
                                store(h, r)
                                if h + 1 < H8:
                                    exps(h + 1, r)
                            if h == 1:
                                value_group(1)
                        result(st, s)

                    def ternary(st, s):
                        turned(st, s)
                        for q in range(2):
                            act.wait_ge(*after(f"sc{q}", st, s))
                            if q == 0:
                                wait_big(s)
                            for h in range(2):
                                f = 2 * q + h
                                ins = nc.scalar.activation(big[:, s, f * SEQ:(f + 1) * SEQ], sc[:, q, h, :], ACT.Relu,
                                                           bias=vec("b1_3a", FT)[:, f:f + 1])
                            ins.then_inc(*a.tick("read", f"sc{q}", st, s))
                        result(st, s)

                    for st, s in STAGES:
                        if st in ATT:
                            attention(st, s)
                        elif st in EXPERTS:
                            experts(st)
                        elif st == "F2":
                            self_attention(st, s)
                        else:
                            ternary(st, s)
                    act.wait_ge(*a.now())

                @block.vector
                def _(dve):
                    v = Progress("dve", plan)

                    def norm(st, s):
                        src = xs
                        for again in range(2 if st == "X1" else 1):
                            dve.wait_ge(*v.now())
                            for k in range(TILES):
                                nc.vector.bn_stats(stats[:, s, k, :], src[:, s, k, :]).then_inc(*v.tick())
                            dve.wait_ge(*v.now())
                            for k in range(TILES):
                                nc.vector.bn_aggr(mv[:, s, k, :], stats[:, s, k, :]).then_inc(*v.tick())
                            dve.wait_ge(*v.now())
                            nc.vector.tensor_scalar(ve[:, s, :], mv[:, s, :, 1], EPS, None, ALU.add)\
                                .then_inc(*v.tick("variance", st, s, again))
                            dve.wait_ge(*after("rstd", st, s, again))
                            for k in range(TILES):
                                nc.vector.tensor_scalar(xn[:, s, k, :], src[:, s, k, :], mv[:, s, k, 0:1],
                                                        rstd[:, s, k:k + 1], ALU.subtract, ALU.mult)\
                                    .then_inc(*v.tick("xn", st, s))
                            src = xn

                    def residual(st, s):
                        dve.wait_ge(*after("tb0", st, s, "y"))
                        nc.vector.tensor_tensor(xs[:, s].rearrange("p t d -> p (t d)"),
                                                xs[:, s].rearrange("p t d -> p (t d)"), tb[:, 0, :], ALU.add)\
                            .then_inc(*v.tick("x done", st, s))
                        plan.labels[("read", "tb0", st, s, "y")] = ("dve", v.count)

                    def attention(st, s):
                        norm(st, s)
                        units = ATT[st] // H8 * TILES

                        def head(p, h):
                            return sc[:, p, h // 4, (h % 4) * KEYS:(h % 4 + 1) * KEYS]

                        def shift(u):
                            p = u % 2
                            scv = sc[:, p, :, 0:4 * KEYS].rearrange("p j (h k) -> p j h k", h=4)
                            dve.wait_ge(*after(f"sc{p}", st, s, u))
                            if st == "X2":
                                for rnd in range(TOP2 // 8):
                                    m8 = m8b if rnd else m8a
                                    base = v.count
                                    for h in range(H8):
                                        src = wk[:, p, h * KEYS:(h + 1) * KEYS] if rnd else head(p, h)
                                        if rnd:
                                            dve.wait_ge(v.plan.sems["dve"], base - H8 + h + 1)
                                        nc.vector.max(m8[:, p, h, :], src).then_inc(*v.tick())
                                    base = v.count
                                    for h in range(H8):
                                        src = wk[:, p, h * KEYS:(h + 1) * KEYS] if rnd else head(p, h)
                                        dve.wait_ge(v.plan.sems["dve"], base - H8 + h + 1)
                                        nc.vector.match_replace(wk[:, p, h * KEYS:(h + 1) * KEYS], m8[:, p, h, :],
                                                                src, TAKEN).then_inc(*v.tick())
                                peak = m8a[:, p, :, 0]
                            else:
                                nc.vector.tensor_reduce(mx[:, p, :].rearrange("p (j h) -> p j h", j=2), scv, AX.X,
                                                        ALU.max).then_inc(*v.tick())
                                peak = mx[:, p, :]
                            dve.wait_ge(*v.now())
                            if u >= 2:
                                dve.wait_ge(*after("tb1", st, s, u - 2))
                            nc.vector.tensor_tensor(
                                ee[:, p, 0:H8 * KEYS].rearrange("p (j h k) -> p j h k", j=2, h=4), scv,
                                peak.rearrange("p (j h) -> p j h", j=2).unsqueeze(3).to_broadcast([P, 2, 4, KEYS]),
                                ALU.subtract).then_inc(*v.tick("shifted", st, s, u))
                            plan.labels[("read", f"sc{p}", st, s, u)] = ("dve", v.count)

                        def total(u):
                            p = u % 2
                            dve.wait_ge(*after("exps", st, s, u))
                            if st == "X2":
                                nc.vector.scalar_tensor_tensor(ee[:, p, 0:H8 * KEYS], wk[:, p, :], TAKEN_BELOW,
                                                               ee[:, p, 0:H8 * KEYS], ALU.is_le, ALU.mult)\
                                    .then_inc(*v.tick())
                                dve.wait_ge(*v.now())
                            nc.vector.tensor_reduce(sums[:, p, :], ee[:, p, 0:H8 * KEYS]
                                                    .rearrange("p (h k) -> p h k", h=H8), AX.X, ALU.add)\
                                .then_inc(*v.tick())
                            dve.wait_ge(*v.now())
                            nc.vector.reciprocal(rs[:, p, :], sums[:, p, :]).then_inc(*v.tick("rsum", st, s, u))

                        shift(0)
                        for u in range(units):
                            if u + 1 < units:
                                shift(u + 1)
                            total(u)
                        residual(st, s)

                    def experts(st):
                        n = EXPERTS[st]
                        for s in range(SLOTS):
                            norm(st, s)
                        for s in range(SLOTS):
                            nc.vector.memset(yT[:, s, :], 0.0).then_inc(*v.tick())
                        for s in range(SLOTS):
                            dve.wait_ge(*after("mb", st, s, "logits"))
                            logits = mb[:, 0:TILES * n].rearrange("p (t e) -> p t e", t=TILES)
                            if st == "F0":
                                dve.wait_ge(*after("norms", st, s))
                                nc.vector.tensor_tensor(lg[:, s, :, 0:E0], logits,
                                                        sq[:, s, :].unsqueeze(2).to_broadcast([P, TILES, E0]),
                                                        ALU.subtract).then_inc(*v.tick("read", "mb", st, s, "logits"))
                                dve.wait_ge(*v.now())
                                for k in range(TILES):
                                    nc.vector.max(m8r[:, s, k, :], lg[:, s, k, 0:E0]).then_inc(*v.tick())
                                dve.wait_ge(*v.now())
                                nc.vector.tensor_copy(top[:, s, :, 0:TOP0], m8r[:, s, :, 0:TOP0]).then_inc(*v.tick())
                                nc.vector.tensor_tensor(ex[:, s, :, :], lg[:, s, :, 0:E0],
                                                        m8r[:, s, :, 0:1].to_broadcast([P, TILES, E0]),
                                                        ALU.subtract).then_inc(*v.tick("router shifted", st, s))
                                dve.wait_ge(*v.now())
                                for k in range(TILES):
                                    nc.vector.match_replace(lgw[:, s, k, :], top[:, s, k, :], lg[:, s, k, :], TAKEN)\
                                        .then_inc(*v.tick())
                            else:
                                nc.vector.tensor_reduce(den[:, s, :], logits, AX.X, ALU.max).then_inc(*v.tick())
                                dve.wait_ge(*v.now())
                                nc.vector.tensor_tensor(ex[:, s, :, 0:E1], logits,
                                                        den[:, s, :].unsqueeze(2).to_broadcast([P, TILES, E1]),
                                                        ALU.subtract).then_inc(*v.tick("router shifted", st, s))
                                plan.labels[("read", "mb", st, s, "logits")] = ("dve", v.count)
                        for s in range(SLOTS):
                            e = ex[:, s, :, 0:n]
                            dve.wait_ge(*after("router exps", st, s))
                            dve.wait_ge(*v.now())
                            if st == "F0":
                                nc.vector.scalar_tensor_tensor(e, lgw[:, s, :, 0:E0], TAKEN_BELOW, e, ALU.is_le,
                                                               ALU.mult).then_inc(*v.tick())
                                dve.wait_ge(*v.now())
                            nc.vector.tensor_reduce(den[:, s, :], e, AX.X, ALU.add).then_inc(*v.tick())
                            dve.wait_ge(*v.now())
                            nc.vector.reciprocal(rden[:, s, :], den[:, s, :]).then_inc(*v.tick())
                            dve.wait_ge(*v.now())
                            dst = cw[:, s, :, :] if st == "F0" else pr[:, :, s * E1:(s + 1) * E1]
                            nc.vector.tensor_tensor(dst, e, rden[:, s, :].unsqueeze(2).to_broadcast([P, TILES, n]),
                                                    ALU.mult).then_inc(*v.tick("expert probs", st))
                            if st == "F0":
                                split([c3[:, s, :, k * E0:(k + 1) * E0] for k in range(3)], cw[:, s, :, :],
                                      ("gate parts", st, s))
                        if st == "F1":
                            dve.wait_ge(*after("read", "mb", st, "probs"))
                            for rnd in range(TOP1 // 8):
                                src = wkT if rnd else prT
                                dve.wait_ge(*v.now())
                                nc.vector.max(m16[:, :], src[:, :]).then_inc(*v.tick())
                                dve.wait_ge(*v.now())
                                nc.vector.match_replace(wkT[:, :], m16[:, :], src[:, :], TAKEN).then_inc(*v.tick())
                            dve.wait_ge(*v.now())
                            nc.vector.scalar_tensor_tensor(prT[:, :], wkT[:, :], TAKEN_BELOW, prT[:, :], ALU.is_le,
                                                           ALU.mult).then_inc(*v.tick())
                            split([parts[:, k, :] for k in range(3)], prT[:, :], ("parts", st))
                        first = v.count
                        with dve.Fori(0, n // 2) as i:
                            for j in range(2):
                                for s in range(SLOTS):
                                    dve.wait_ge(*after_in(st, i, "gate row", st, SLOTS * j + s))
                                    dve.wait_ge(*after_in(st, i, "expert out", st, SLOTS * j + s))
                                    nc.vector.scalar_tensor_tensor(tmp[:, s, :], tb[:, s, :],
                                                                   we[:, j, EXPERT_COLS - 1:EXPERT_COLS], cb[:, s, :],
                                                                   ALU.add, ALU.mult)\
                                        .then_inc(*v.tick("gated", st, j, s))
                                    dve.wait_ge(*v.now_in(st, i))
                                    nc.vector.tensor_tensor(yT[:, s, :], yT[:, s, :], tmp[:, s, :], ALU.add)\
                                        .then_inc(*v.tick())
                        v.loop_ends(st, first, n // 2)
                        for b in range(2):
                            plan.labels[("read", f"tb{b}", st, "loop", f"tb{b}")] = ("dve", v.count)
                        for s in range(SLOTS):
                            plan.labels[("yT", st, s)] = ("dve", v.count)
                        for s in range(SLOTS):
                            residual(st, s)

                    def split(dsts, src, label):
                        for k, d in enumerate(dsts):
                            dve.wait_ge(*v.now())
                            nc.vector.tensor_copy(d, src).then_inc(*v.tick(*(label if k == 2 else ())))
                            if k < 2:
                                dve.wait_ge(*v.now())
                                nc.vector.tensor_tensor(src, src, d, ALU.subtract).then_inc(*v.tick())

                    def self_attention(st, s):
                        norm(st, s)

                        def maxima(h, r):
                            dve.wait_ge(*after(f"sc{r}", st, s, h))
                            nc.vector.tensor_reduce(mx[:, r, 0:2], sc[:, r, :, :], AX.X, ALU.max, negate=True)\
                                .then_inc(*v.tick("maxima", st, s, h, r))

                        def weigh(h, r):
                            dve.wait_ge(*after("exps", st, s, h, r))
                            nc.vector.reciprocal(rg[:, r, :], dn[:, r, :]).then_inc(*v.tick())
                            dve.wait_ge(*v.now())
                            nc.vector.tensor_tensor(rg[:, r, :], rg[:, r, :], gt[:, s, 2 * r:2 * r + 2, h], ALU.mult)\
                                .then_inc(*v.tick())
                            dve.wait_ge(*v.now())
                            for i in range(2):
                                e = ee[:, r, i * SEQ:(i + 1) * SEQ]
                                nc.vector.tensor_scalar(e, e, rg[:, r, i:i + 1], None, ALU.mult)\
                                    .then_inc(*v.tick("probs", st, s, h, r))

                        def store(h, r):
                            dve.wait_ge(*after("tb1", st, s, h, r))
                            if r == 0:
                                dve.wait_ge(*after("read", "tb0", st, s, h, r))
                            dst = big[:, h % 2, 0:TILES * SEQ].rearrange("p (k q) -> p k q", k=TILES)
                            nc.vector.tensor_copy(dst[:, :, (2 * r + 1) * P:(2 * r + 2) * P],
                                                  tb[:, 1, :].rearrange("p (k q) -> p k q", k=TILES))\
                                .then_inc(*v.tick("read", "tb1", st, s, h, r))

                        maxima(0, 0)
                        maxima(0, 1)
                        g = sg[:, s, :, 0:H8]
                        dve.wait_ge(*after("read", "mb", st, s, "gate"))
                        nc.vector.tensor_scalar(g, g, 1.0, None, ALU.add).then_inc(*v.tick())
                        dve.wait_ge(*v.now())
                        nc.vector.reciprocal(g, g).then_inc(*v.tick())
                        dve.wait_ge(*v.now())
                        for k in range(TILES):
                            nc.vector.max(m8r[:, s, k, :], sg[:, s, k, 0:H8]).then_inc(*v.tick())
                        dve.wait_ge(*v.now())
                        nc.vector.tensor_copy(topF[:, s, :, 0:TOPF2], m8r[:, s, :, 0:TOPF2]).then_inc(*v.tick())
                        dve.wait_ge(*v.now())
                        for k in range(TILES):
                            nc.vector.match_replace(sgw[:, s, k, :], topF[:, s, k, :], sg[:, s, k, :], TAKEN)\
                                .then_inc(*v.tick())
                        dve.wait_ge(*v.now())
                        nc.vector.scalar_tensor_tensor(gt[:, s, :, :], sgw[:, s, :, 0:H8], TAKEN_BELOW, g, ALU.is_le,
                                                       ALU.mult).then_inc(*v.tick("gates", st, s))
                        dve.wait_ge(*v.now())
                        weigh(0, 0)
                        weigh(0, 1)
                        for h in range(H8):
                            for r in range(2):
                                store(h, r)
                                if h + 1 < H8:
                                    maxima(h + 1, r)
                                    weigh(h + 1, r)
                        residual(st, s)

                    def ternary(st, s):
                        norm(st, s)
                        residual(st, s)

                    for s in range(SLOTS):
                        dve.wait_ge(x_in[s], 16)
                    for st, s in STAGES:
                        if st in ATT:
                            attention(st, s)
                        elif st in EXPERTS:
                            experts(st)
                        elif st == "F2":
                            self_attention(st, s)
                        else:
                            ternary(st, s)
                    dve.wait_ge(*v.now())

                @block.gpsimd
                def _(pool):
                    g = Progress("pool", plan)

                    def keys(st, s):
                        batch = turn * SLOTS + s
                        prev = {"X1": "X0", "X2": "X1", "X3": "X2"}.get(st)
                        if prev:
                            pool.wait_ge(*after("values", prev, s, ATT[prev] // H8 - 1))
                        n = ATT[st]
                        dst = kb[:, s, 0:n * KEYS].rearrange("p (h k) -> p h k", h=n)
                        src = ctxv[st][:, bass.ds(batch * KEYS, KEYS)] if st in HEADROWS else \
                            small_("ctxT")[:, bass.ds(batch * KEYS, KEYS)]
                        nc.gpsimd.tensor_copy(ctxb[:, s, :], src).then_inc(*g.tick("ctx cols", st, s))
                        if st in HEADROWS:
                            nc.gpsimd.tensor_tensor(
                                dst, ctxk[st][:, bass.ds(batch * KEYS, KEYS)].unsqueeze(1).to_broadcast([P, n, KEYS]),
                                headmask[:, :].unsqueeze(2).to_broadcast([P, n, KEYS]), ALU.mult)\
                                .then_inc(*g.tick("keys", st, s))
                        else:
                            src = keys1 if st == "X1" else keys3
                            nc.gpsimd.tensor_copy(dst, src[:, batch]).then_inc(*g.tick("keys", st, s))

                    def norm(st, s):
                        for again in range(2 if st == "X1" else 1):
                            pool.wait_ge(*after("variance", st, s, again))
                            nc.gpsimd.tensor_tensor(rstd[:, s, :], ve[:, s, :], minus_half[:, :], ALU.pow)\
                                .then_inc(*g.tick("rstd", st, s, again))

                    for st, s in STAGES:
                        if st in ATT:
                            keys(st, s)
                        for k in slots_of(s):
                            norm(st, k)
                        if st in ATT:
                            for u in range(ATT[st] // H8 * TILES):
                                p = u % 2
                                pool.wait_ge(*after("rsum", st, s, u))
                                e = ee[:, p, 0:H8 * KEYS].rearrange("p (h k) -> p h k", h=H8)
                                nc.gpsimd.tensor_tensor(e, e, rs[:, p, :].unsqueeze(2).to_broadcast([P, H8, KEYS]),
                                                        ALU.mult).then_inc(*g.tick("probs", st, s, u))
                    pool.wait_ge(*g.now())


def kernel(**inputs):
    import numpy as np
    import concourse.bacc as bacc
    from concourse.bass_utils import run_bass_kernel_spmd

    a = {k: np.asarray(v) for k, v in inputs.items()}
    col = lambda v: np.asarray(v, np.float32).reshape(P, 1)
    vecs = [a["L0_xattn_bq"], a["L0_xattn_bk"], a["L0_xattn_bv"], a["L0_xattn_bo"],
            a["L2_xattn_bq"], a["L2_xattn_bk"], a["L2_xattn_bv"], a["L2_xattn_bo"],
            a["L1_xattn_ln_gamma"], a["L1_xattn_ln_beta"], a["L1_xattn_b_out"], a["L3_xattn_bo"], a["L3_ffn_b2"],
            np.broadcast_to(a["L1_xattn_gate"], (P,))] + list(a["L3_ffn_b1"].reshape(FT, P))
    tiles = lambda w: np.ascontiguousarray(w.reshape(FT, P, D).transpose(1, 0, 2)).reshape(P, FT * D)
    small = np.concatenate(
        [col(v) for v in vecs] + [a["ctx_1024"].reshape(CTX, D).T]
        + [a[f"L{n}_xattn_{w}"].T for n in (0, 2) for w in ("Wq", "Wk", "Wv", "Wo")]
        + [a["L0_ffn_keys"].T, a["L0_ffn_rw"].T, a["L1_ffn_gate_w"].T, a["L2_ffn_Ws"],
           a["L3_ffn_W1"].T, tiles(a["L3_ffn_W2"].T)], axis=1)
    assert small.shape == (P, SMALL_COLS)

    def head_pack(wq, wk, wv, wo, n):
        cut = lambda w: w.reshape(D, n, DH).transpose(2, 1, 0).reshape(DH, n * D)
        return np.stack([cut(wq), cut(wk), cut(wv), wo.reshape(n, DH, D).transpose(1, 0, 2).reshape(DH, n * D)])

    wkv = a["L1_xattn_w_kv"]
    heads1 = head_pack(a["L1_xattn_w_q"], wkv[:, :H16 * DH], wkv[:, H16 * DH:], a["L1_xattn_w_out"], H16)
    heads3 = head_pack(a["L3_xattn_Wq"], a["L3_xattn_Wk"], a["L3_xattn_Wv"], a["L3_xattn_Wo"], H8)
    wkv = a["L2_ffn_Wkv"]
    headsF = head_pack(a["L2_ffn_Wq"], wkv[:, :H8 * DH], wkv[:, H8 * DH:], a["L2_ffn_Wo"].reshape(H8 * DH, D), H8)

    def expert_pack(w1, w2, b1, b2):
        n = w1.shape[0]
        return np.concatenate([w1, w2.reshape(n, FT, P, D).transpose(0, 2, 1, 3).reshape(n, P, FT * D),
                               b1.reshape(n, FT, P).transpose(0, 2, 1), b2.reshape(n, D, 1)], axis=2)

    experts0 = expert_pack(a["L0_ffn_w1"].transpose(0, 2, 1), a["L0_ffn_w2"].transpose(0, 2, 1), a["L0_ffn_b1"],
                           a["L0_ffn_b2"])
    experts1 = expert_pack(a["L1_ffn_w1"], a["L1_ffn_w2"], np.zeros((E1, FT * P), np.float32),
                           np.zeros((E1, D), np.float32))
    rows = np.zeros((1 + H8, D), np.float32)
    rows[0, :E0] = a["L0_ffn_rb"]
    rows[1:] = a["L2_ffn_bo"]
    arrays = {k: np.ascontiguousarray(v) for k, v in dict(
        x=a["x"], small=small, heads1=heads1, heads3=heads3, headsF=headsF, experts0=experts0, experts1=experts1,
        rows=rows).items()}

    plan = Plan()
    for _ in range(2):
        nc = bacc.Bacc("TRN2", target_bir_lowering=False, num_devices=1)
        args = [nc.dram_tensor(f"in_{k}", v.shape, F32, kind="ExternalInput").ap() for k, v in arrays.items()]
        out = nc.dram_tensor("out_x", (BATCH, SEQ, D), F32, kind="ExternalOutput").ap()
        network(nc, plan, *args, out)
    r = run_bass_kernel_spmd(nc, [{f"in_{k}": v for k, v in arrays.items()}], core_ids=[0])
    return r.results[0]["out_x"]
```

```python
from contextlib import ExitStack

import concourse.bass as bass
from concourse import mybir

F32 = mybir.dt.float32
BF16 = mybir.dt.bfloat16
ALU = mybir.AluOpType
ACT = mybir.ActivationFunctionType
AX = mybir.AxisListType

P = 128
BATCH, SEQ, D = 4, 512, 128
TILES = SEQ // P
KEYS = 77
CTX = BATCH * KEYS
THREADS = 2
H16, H8 = 16, 8
DH = 64
FT = 4
E0, E1 = 16, 8
TOP0, TOP1, TOP2, TOPF2 = 4, 128, 32, 3
EPS = 1e-5
TAKEN = -3.0e38
TAKEN_BELOW = -2.9e38
FILLER = 3.0e38
ROUND = 1.5 * 2.0 ** 23

VEC = {n: i for i, n in enumerate(
    ["bq0", "bk0", "bv0", "bo0", "bq2", "bk2", "bv2", "bo2", "gamma", "beta", "bo1", "bo3", "b2_3", "gate",
     "b1_3a", "b1_3b", "b1_3c", "b1_3d"])}
SMALL = {}
_at = 0
for _n, _w in (("vec", len(VEC)), ("ctxT", CTX), ("wq0", D), ("wk0", D), ("wv0", D), ("wo0", D), ("wq2", D),
               ("wk2", D), ("wv2", D), ("wo2", D), ("keysT", E0), ("rwT", E0), ("gwT", E1), ("wsT", H8),
               ("w1_3", FT * P), ("w2_3", FT * P)):
    SMALL[_n] = (_at, _w)
    _at += _w
SMALL_COLS = _at
EXPERT_COLS = 2 * FT * P + FT + 1
W1_COLS = FT * P + FT
UNIT = H8 * KEYS
TOPK_STEPS = TOP1 // 8 // 2

NET = ("X0", "F0", "X1", "F1", "X2", "F2", "X3", "F3")
ATT = {"X0": H16, "X1": H16, "X2": H16, "X3": H8}
HEADROWS = ("X0", "X2")
SCALE = {"X0": 8 ** -0.5, "X1": DH ** -0.5, "X2": 8 ** -0.5, "X3": DH ** -0.5}
EXPERTS = {"F0": E0, "F1": E1}
SUBSTEPS = {st: TOP2 // 8 if st == "X2" else 1 for st in ATT}
NORM_STEPS = {st: 2 if st == "X1" else 1 for st in NET}


def steps_of(st):
    if st in ATT:
        return NORM_STEPS[st] + 2 + 1 + (ATT[st] // H8 * TILES + 2) * SUBSTEPS[st] + 2
    if st in EXPERTS:
        return NORM_STEPS[st] + 2 + 2 + (TOPK_STEPS + 1 + EXPERTS[st] + 3 if st == "F1" else EXPERTS[st] + 1) + 2
    if st == "F2":
        return NORM_STEPS[st] + 2 + 2 + 2 * H8 + 2 + 2
    return NORM_STEPS[st] + 2 + 3


STEPS = {st: steps_of(st) for st in NET}
WEIGHT = {"X0": 4, "F0": 7.3, "X1": 4.4, "F1": 3.6, "X2": 3.4, "F2": 4.3, "X3": 4, "F3": 3.5}
LIGHT = 3.6
LAG, LAG_AT = 37, "F0"
CATCH, CATCH_AT = 24, "F3"


def step_weights(st):
    first = NORM_STEPS[st] + 2 + (2 + (TOPK_STEPS + 1 if st == "F1" else 0) if st in EXPERTS else 1)
    return [LIGHT if k < first or k >= STEPS[st] - 2 else WEIGHT[st] for k in range(STEPS[st])]


def merge_order():
    weights = [step_weights(st) for st in NET]
    waits = {(1, LAG_AT): LAG, (0, CATCH_AT): CATCH}
    waits = {(s, sum(STEPS[n] for n in NET[:NET.index(st)])): w for (s, st), w in waits.items()}
    weights = [w for stage in weights for w in stage]
    at, done, order = [0, 0], [0, 0], []
    while min(done) < len(weights):
        s = min((k for k in range(THREADS) if done[k] < len(weights)), key=lambda k: at[k])
        wait = waits.pop((s, done[s]), 0)
        if wait:
            at[s] += wait
            continue
        at[s] += weights[done[s]]
        done[s] += 1
        order.append(s)
    return order


ORDER = merge_order()


def network_of(s, attention, experts, self_attention, ternary):
    for st in NET:
        run = attention if st in ATT else experts if st in EXPERTS else self_attention if st == "F2" else ternary
        count = 0
        for _ in run(st, s):
            count += 1
            yield
        assert count == STEPS[st], (st, count, STEPS[st])


def merged(thread):
    threads = [thread(s) for s in range(THREADS)]
    for s in ORDER:
        next(threads[s])
    for s in range(THREADS):
        assert next(threads[s], None) is None


class Plan:

    def __init__(self):
        self.labels = {}

    def start(self, sems):
        self.sems = sems

    def after(self, *label):
        engine, count = self.labels.get(label, ("pe", 0))
        return self.sems[engine], count


class Progress:
    def __init__(self, name, plan):
        self.name, self.plan, self.count = name, plan, 0

    def tick(self, *label):
        self.count += 1
        if label:
            self.plan.labels[label] = (self.name, self.count)
        return self.plan.sems[self.name], 1

    def now(self):
        return self.plan.sems[self.name], self.count


def network(nc, plan, x, small, heads1, heads3, headsF, experts0, experts1, rows, out):
    with ExitStack() as ctx:
        def sb(name, shape, dt=F32):
            return ctx.enter_context(nc.sbuf_tensor(name, shape, dt))

        def sem(name):
            return ctx.enter_context(nc.semaphore(name))

        sm = sb("small_weights", [P, SMALL_COLS])
        ident = sb("ident", [P, P])
        identb = sb("identb", [P, P], BF16)
        ones = sb("ones", [P, P])
        headmask = sb("headmask", [P, H16])
        sel = sb("sel", [P, E0, P], BF16)
        onesb = sb("onesb", [P, P], BF16)
        upto = sb("upto", [P, P], BF16)
        place = sb("place", [P, P])
        ctxk = {"X0": sb("kT0", [P, CTX]), "X2": sb("kT2", [P, CTX])}
        ctxv = {"X0": sb("vT0", [P, CTX]), "X2": sb("vT2", [P, CTX])}
        C = {"X0": sb("C0", [P, H16 * D]), "X1": sb("C1", [P, H16 * D]), "X2": sb("C2", [P, H16 * D]),
             "X3": sb("C3", [P, H8 * D])}
        AF = sb("AF", [P, H8 * D])
        CF = sb("CF", [P, H8 * D])
        W1q = sb("W1q", [P, FT * P])
        W2q = sb("W2q", [P, FT * P])
        R0 = sb("R0", [P, E0])
        c0row = sb("c0row", [1, E0])
        rbrow = sb("rbrow", [1, E0])
        boF = sb("boF", [H8, D])
        tg = sb("tanh_gate", [P, 1])
        bo1g = sb("bo1g", [P, 1])
        minus_half = sb("minus_half", [P, TILES])
        qsum = sb("qsum", [P, 2])
        qinv = sb("qinv", [P, 2])

        big = sb("big", [P, THREADS, H8 * SEQ])
        vp = sb("values", [P, THREADS, H16 * D])
        ee = sb("numerators", [P, THREADS, 4 * SEQ])
        kb = sb("keys", [P, THREADS, H16 * KEYS])
        wk = sb("topk_work", [P, THREADS, 2, H8 * KEYS])
        w1s = sb("expert_w1", [P, THREADS, 2, W1_COLS])
        w2s = sb("expert_w2", [P, THREADS, 2, EXPERT_COLS - W1_COLS])
        kpt = sb("keysF", [P, THREADS, 2, SEQ])
        xs = sb("x_res", [P, THREADS, TILES, D])
        xn = sb("xn", [P, THREADS, TILES, D])
        xnT = sb("xnT", [P, THREADS, SEQ])
        yT = sb("yT", [P, THREADS, SEQ])
        cb = sb("gate_rows", [P, THREADS, SEQ])
        qT = cb
        tmp = sb("gated", [P, THREADS, SEQ])
        ctxb = sb("ctx_cols", [P, THREADS, KEYS])
        stats = sb("stats", [P, THREADS, TILES, 6])
        mv = sb("mv", [P, THREADS, TILES, 2])
        ve = sb("ve", [P, THREADS, TILES])
        rstd = sb("rstd", [P, THREADS, TILES])
        mx = sb("mx", [P, THREADS, 2, H8])
        sums = sb("sums", [P, THREADS, 2, H8])
        rs = sb("rs", [P, THREADS, 2, H8])
        m8a = sb("m8a", [P, THREADS, H8, 8])
        minus_peak = sb("minus_peak", [P, THREADS, H8])
        m8b = sb("m8b", [P, THREADS, H8, 8])
        sq = sb("sq", [P, THREADS, TILES])
        lg = sb("lg", [P, THREADS, TILES, E0 + 4])
        lgw = sb("lgw", [P, THREADS, TILES, E0 + 4])
        m8r = sb("m8r", [P, THREADS, TILES, 8])
        top = sb("top", [P, THREADS, TILES, 8])
        ex = sb("ex", [P, THREADS, TILES, E0])
        den = sb("den", [P, THREADS, TILES])
        rden = sb("rden", [P, THREADS, TILES])
        cw = sb("cw", [P, THREADS, TILES, E0])
        c3 = sb("c3", [P, THREADS, TILES, P], BF16)
        c3T = sb("c3T", [P, THREADS, SEQ], BF16)
        prT = [kpt[0:E1, s, 0, :] for s in range(THREADS)]
        wkT = [kpt[0:E1, s, 1, :] for s in range(THREADS)]
        m16 = sb("m16", [E1, THREADS, 8])
        pr = sb("pr", [P, THREADS, TILES, E1])
        taken = sb("taken", [P, THREADS, TILES, E1], BF16)
        slot = sb("slot", [P, THREADS, TILES, E1])
        hot = [ee[:, s, 0:2 * SEQ].rearrange("p (j k q) -> p j k q", j=2, k=TILES) for s in range(THREADS)]
        hotg = [ee[:, s, 2 * SEQ:4 * SEQ].rearrange("p (j k q) -> p j k q", j=2, k=TILES) for s in range(THREADS)]
        hotT = [vp[:, s, 0:2 * SEQ].rearrange("p (j q) -> p j q", j=2) for s in range(THREADS)]
        xg = [vp[:, s, 2 * SEQ:2 * SEQ + 2 * P].rearrange("p (j q) -> p j q", j=2) for s in range(THREADS)]
        og = [vp[:, s, 2 * SEQ + 2 * P:2 * SEQ + 4 * P].rearrange("p (j q) -> p j q", j=2) for s in range(THREADS)]
        sg = sb("sg", [P, THREADS, TILES, H8 + 5])
        sgw = sb("sgw", [P, THREADS, TILES, H8 + 5])
        topF = sb("topF", [P, THREADS, TILES, 8])
        gt = sb("gt", [P, THREADS, TILES, H8])
        gtT = tmp[0:H8, :, :]
        dn = sb("dn", [P, THREADS, 2, 2])
        rg = sb("rg", [P, THREADS, 2, 2])

        sc = ctx.enter_context(nc.psum_tensor("scores", [P, THREADS, 2, SEQ], F32))
        tb = ctx.enter_context(nc.psum_tensor("turned", [P, THREADS, SEQ], F32))
        yb = ctx.enter_context(nc.psum_tensor("result", [P, THREADS, SEQ], F32))

        sems = {n: sem(f"{n}_progress") for n in ("pe", "act", "dve", "pool")}
        x_in = [sem(f"x_in{s}") for s in range(THREADS)]
        x_out = [sem(f"x_out{s}") for s in range(THREADS)]
        w_in = {(s, part, j): sem(f"thread{s}_w{part}_in{j}") for s in range(THREADS) for part in (1, 2)
                for j in range(2)}
        keys_in = [sem(f"keys_in{s}") for s in range(THREADS)]
        keys_out = [sem(f"keys_out{j}") for j in range(2)]
        small_in = sem("small_in")
        rows_in = sem("rows_in")
        heads_in = {pair + n: sem(f"heads_{pair}{n}_in") for pair in "AC" for n in "13F"}
        every = list(sems.values()) + x_in + x_out + list(w_in.values()) + keys_in + keys_out \
            + [small_in, rows_in] + list(heads_in.values())
        plan.start(sems)
        after = plan.after

        keys_dram = {st: nc.dram_tensor(f"keys_{st}", [BATCH, P, ATT[st] * KEYS], F32, kind="Internal").ap()
                     for st in ("X1", "X3")}

        def small_(name):
            a, w = SMALL[name]
            return sm[:, a:a + w]

        def vec(name, n=1):
            return sm[:, VEC[name]:VEC[name] + n]

        hp1 = [big[0:DH, k // 2, (k % 2) * 2048:(k % 2) * 2048 + 2048] for k in range(4)]
        hp3 = [vp[0:DH, k // 2, (k % 2) * 1024:(k % 2) * 1024 + 1024] for k in range(4)]
        hpF = [ee[0:DH, k // 2, (k % 2) * 1024:(k % 2) * 1024 + 1024] for k in range(4)]

        GROUPS = ([("A1", hp1, g) for g in range(4)] + [("C1", hp1, g) for g in range(4)]
                  + [("A3", hp3, g) for g in range(2)] + [("C3", hp3, g) for g in range(2)]
                  + [("AF", hpF, g) for g in range(2)] + [("CF", hpF, g) for g in range(2)])
        KEY_GROUPS = [n for n, g in enumerate(GROUPS) if g[0] in ("A1", "A3")]
        A1 = wk[:, 0, :, :].rearrange("p a b -> p (a b)")
        with nc.Block() as block:
            @block.sync
            def _(sp):
                sp.dma_start(sm[:, :], small).then_inc(small_in, 16)
                for k in range(4):
                    sp.dma_start(hp1[k], heads1[k]).then_inc(heads_in["AACC"[k] + "1"], 16)
                for k in range(4):
                    sp.dma_start(hp3[k], heads3[k]).then_inc(heads_in["AACC"[k] + "3"], 16)
                for k in range(4):
                    sp.dma_start(hpF[k], headsF[k]).then_inc(heads_in["AACC"[k] + "F"], 16)
                for m, n in enumerate(KEY_GROUPS):
                    kind, _, grp = GROUPS[n]
                    sp.wait_ge(*after("pro keys out", n, 3))
                    sp.dma_start(keys_dram["X1" if kind == "A1" else "X3"]
                                 .rearrange("b p c -> p b c")[:, :, 4 * grp * KEYS:4 * (grp + 1) * KEYS],
                                 kb[:, m % 2, :].rearrange("p (b c) -> p b c", b=BATCH)).then_inc(keys_out[m % 2], 16)
                for j in range(2):
                    sp.wait_ge(keys_out[j], 16 * len(KEY_GROUPS) // 2)

            @block.gpsimd
            def _(pool):
                g = Progress("pool", plan)
                nc.gpsimd.memset(ident[:, :], 0.0).then_inc(*g.tick())
                nc.gpsimd.memset(identb[:, :], 0.0).then_inc(*g.tick())
                nc.gpsimd.memset(headmask[:, :], 1.0).then_inc(*g.tick())
                nc.gpsimd.memset(sel[:, :, :], 0.0).then_inc(*g.tick())
                nc.gpsimd.memset(onesb[:, :], 1.0).then_inc(*g.tick())
                nc.gpsimd.memset(upto[:, :], 1.0).then_inc(*g.tick())
                pool.wait_ge(*g.now())
                nc.gpsimd.affine_select(out=upto[:, :], in_=upto[:, :], compare_op=ALU.is_ge, fill=0.0, base=0,
                                        pattern=[[1, P]], channel_multiplier=-1).then_inc(*g.tick("upto"))
                for m in (ident, identb):
                    nc.gpsimd.affine_select(out=m[:, :], in_=m[:, :], compare_op=ALU.not_equal, fill=1.0, base=0,
                                            pattern=[[-1, P]], channel_multiplier=1).then_inc(*g.tick("ident"))
                nc.gpsimd.affine_select(out=headmask[:, :], in_=headmask[:, :], compare_op=ALU.is_ge, fill=0.0,
                                        base=0, pattern=[[-8, H16]], channel_multiplier=1).then_inc(*g.tick())
                pool.wait_ge(*g.now())
                nc.gpsimd.affine_select(out=headmask[:, :], in_=headmask[:, :], compare_op=ALU.is_ge, fill=0.0,
                                        base=7, pattern=[[8, H16]], channel_multiplier=-1)\
                    .then_inc(*g.tick("headmask"))
                for k in range(3):
                    nc.gpsimd.affine_select(out=sel[:, :, :], in_=sel[:, :, :], compare_op=ALU.not_equal, fill=1.0,
                                            base=-E0 * k, pattern=[[-1, E0], [0, P]], channel_multiplier=1)\
                        .then_inc(*g.tick())
                    pool.wait_ge(*g.now())
                pool.wait_ge(small_in, 16)
                for st, w in (("X0", "wo0"), ("X2", "wo2")):
                    nc.gpsimd.tensor_tensor(
                        C[st][:, :].rearrange("p (h e) -> p h e", h=H16),
                        small_(w).unsqueeze(1).to_broadcast([P, H16, D]),
                        headmask[:, :].unsqueeze(2).to_broadcast([P, H16, D]), ALU.mult).then_inc(*g.tick())
                pool.wait_ge(*g.now())
                pool.wait_ge(*g.now())

            @block.scalar
            def _(act):
                a = Progress("act", plan)
                act.dma_start(rbrow[:, :], rows[0:1, 0:E0]).then_inc(rows_in, 16)
                act.dma_start(boF[:, :], rows[1:1 + H8, :]).then_inc(rows_in, 16)
                act.wait_ge(small_in, 16)
                nc.scalar.activation(tg[:, :], vec("gate"), ACT.Tanh).then_inc(*a.tick("tanh"))
                for n, (dst, b) in enumerate(((ctxk["X0"], "bk0"), (ctxv["X0"], "bv0"),
                                              (ctxk["X2"], "bk2"), (ctxv["X2"], "bv2"))):
                    act.wait_ge(*after("pro ctx", n))
                    nc.scalar.activation(dst[:, :], sc[:, n // 2, n % 2, 0:CTX], ACT.Identity, bias=vec(b))\
                        .then_inc(*a.tick("pro ctx out", n))
                for n, (kind, _, grp) in enumerate(GROUPS):
                    act.wait_ge(*after("pro group", n))
                    if kind in ("A1", "A3"):
                        if n >= 2:
                            act.wait_ge(*after("pro group used", max(0, n - 2)))
                        act_dst = A1[:, (n % 2) * 512:(n % 2) * 512 + 512]
                    else:
                        act_dst = {"C1": C["X1"], "C3": C["X3"], "AF": AF, "CF": CF}[kind][:, grp * 512:grp * 512 + 512]
                    scale = DH ** -0.5 if kind == "AF" else 1.0
                    nc.scalar.activation(act_dst, tb[:, n % 2, :], ACT.Copy, scale=scale)\
                        .then_inc(*a.tick("pro group out", n))
                act.wait_ge(*a.now())

            @block.vector
            def _(dve):
                v = Progress("dve", plan)
                nc.vector.memset(ones[:, :], 1.0).then_inc(*v.tick("ones"))
                nc.vector.memset(minus_half[:, :], -0.5).then_inc(*v.tick())
                nc.vector.memset(c3[:, :, :, :], 0.0).then_inc(*v.tick())
                nc.vector.memset(c3T[:, :, :], 0.0).then_inc(*v.tick())
                nc.vector.memset(top[:, :, :, :], FILLER).then_inc(*v.tick())
                nc.vector.memset(topF[:, :, :, :], FILLER).then_inc(*v.tick())
                nc.vector.memset(lg[:, :, :, :], FILLER).then_inc(*v.tick())
                nc.vector.memset(sg[:, :, :, :], FILLER).then_inc(*v.tick())
                dve.wait_ge(small_in, 16)
                nc.vector.scalar_tensor_tensor(R0[:, :], small_("keysT"), 2.0, small_("rwT"), ALU.mult, ALU.add)\
                    .then_inc(*v.tick())
                nc.vector.tensor_tensor(lgw[:, 0, 0, 0:E0], small_("keysT"), small_("keysT"), ALU.mult)\
                    .then_inc(*v.tick("key squares"))
                dve.wait_ge(*after("key norms"))
                dve.wait_ge(rows_in, 32)
                nc.vector.tensor_tensor(c0row[:, :], rbrow[:, :], tb[0:1, 0, 0:E0], ALU.subtract).then_inc(*v.tick())
                dve.wait_ge(*after("places"))
                nc.vector.tensor_copy(place[:, :], tb[:, 1, 0:P]).then_inc(*v.tick("place"))
                dve.wait_ge(*after("tanh"))
                nc.vector.tensor_tensor(bo1g[:, :], vec("bo1"), tg[:, :], ALU.mult).then_inc(*v.tick())
                for k, w in enumerate(("w1_3", "w2_3")):
                    nc.vector.tensor_reduce(qsum[:, k:k + 1], small_(w), AX.X, ALU.add, apply_absolute_value=True)\
                        .then_inc(*v.tick("abs sums"))
                dve.wait_ge(*after("abs means"))
                nc.vector.tensor_scalar(qinv[:, :], yb[:, 0, 0:2], 1.0 / (D * FT * P), EPS, ALU.mult, ALU.add)\
                    .then_inc(*v.tick())
                dve.wait_ge(*v.now())
                nc.vector.reciprocal(qinv[:, :], qinv[:, :]).then_inc(*v.tick())
                dve.wait_ge(*v.now())
                for k, (w, dst) in enumerate((("w1_3", W1q), ("w2_3", W2q))):
                    nc.vector.tensor_scalar(dst[:, :], small_(w), qinv[:, k:k + 1], 1.0, ALU.mult, ALU.min)\
                        .then_inc(*v.tick())
                    dve.wait_ge(*v.now())
                    nc.vector.tensor_scalar(dst[:, :], dst[:, :], -1.0, ROUND, ALU.max, ALU.add).then_inc(*v.tick())
                    dve.wait_ge(*v.now())
                    nc.vector.tensor_scalar(dst[:, :], dst[:, :], -ROUND, None, ALU.add).then_inc(*v.tick())
                for m, n in enumerate(KEY_GROUPS):
                    if m >= 2:
                        dve.wait_ge(keys_out[m % 2], 16 * (m // 2))
                    for i in range(4):
                        dve.wait_ge(*after("pro keys", n, i))
                        nc.vector.tensor_copy(
                            kb[:, m % 2, :].rearrange("p (b h k) -> p b h k", b=BATCH, h=4)[:, :, i, :],
                            sc[:, i // 2, i % 2, 0:CTX].rearrange("p (b k) -> p b k", b=BATCH))\
                            .then_inc(*v.tick("pro keys out", n, i))
                dve.wait_ge(*v.now())

            @block.tensor
            def _(pe):
                t = Progress("pe", plan)
                pe.wait_ge(small_in, 16)
                for n, w in enumerate(("wk0", "wv0", "wk2", "wv2")):
                    nc.tensor.matmul(sc[:, n // 2, n % 2, 0:CTX], small_(w), small_("ctxT"), start=True, stop=True)\
                        .then_inc(*t.tick("pro ctx", n))
                pe.wait_ge(*after("key squares"))
                nc.tensor.matmul(tb[0:1, 0, 0:E0], ones[:, 0:1], lgw[:, 0, 0, 0:E0], start=True, stop=True)\
                    .then_inc(*t.tick("key norms"))
                pe.wait_ge(*after("upto"))
                nc.tensor.matmul(tb[:, 1, 0:P], onesb[:, :], upto[:, :], start=True, stop=True).then_inc(*t.tick("places"))
                pe.wait_ge(*after("abs sums"))
                nc.tensor.matmul(yb[:, 0, 0:2], ones[:, :], qsum[:, :], start=True, stop=True)\
                    .then_inc(*t.tick("abs means"))

                def keys_of(n):
                    pe.wait_ge(*after("pro group out", n))
                    for i in range(4):
                        if keys_of.last is None:
                            pe.wait_ge(*after("pro ctx out", i))
                        else:
                            pe.wait_ge(*after("pro keys out", keys_of.last, i))
                        ins = nc.tensor.matmul(sc[:, i // 2, i % 2, 0:CTX],
                                               A1[:, (n % 2) * 512 + i * P:(n % 2) * 512 + i * P + P],
                                               small_("ctxT"), start=True, stop=True)
                        ins.then_inc(*t.tick("pro keys", n, i))
                    plan.labels[("pro group used", n)] = ("pe", t.count)
                    keys_of.last = n

                keys_of.last = None
                pe.wait_ge(*after("place"))
                pending = None
                for n, (kind, hp, grp) in enumerate(GROUPS):
                    if n >= 2:
                        pe.wait_ge(*after("pro group out", n - 2))
                    if grp == 0:
                        pe.wait_ge(heads_in[kind], 32)
                    first, second = (1, 0) if kind[0] == "A" else (2, 3)
                    for i in range(4):
                        h = 4 * grp + i
                        ins = nc.tensor.matmul(tb[:, n % 2, i * P:(i + 1) * P], hp[first][:, h * P:(h + 1) * P],
                                               hp[second][:, h * P:(h + 1) * P], start=True, stop=True)
                    ins.then_inc(*t.tick("pro group", n))
                    if pending is not None:
                        keys_of(pending)
                    pending = n if kind in ("A1", "A3") else None
                pe.wait_ge(*t.now())

        def unit(p, k):
            return ee[:, p, (k % 3) * UNIT:(k % 3 + 1) * UNIT]

        def value_bank(s, g, k):
            return ("ab"[k % 2], sc[:, s, k % 2, :]) if g == 0 else ("t", tb[:, s, :])

        with nc.Fori(0, BATCH // THREADS) as turn:
            with nc.Block() as block:
                @block.sync
                def _(sp):
                    for q in every:
                        sp.sem_clear(q)

            with nc.Block() as block:
                @block.sync
                def _(sp):
                    loads = {}

                    def load(s, part, ring, pack, e, a, b):
                        sp.dma_start(ring[:, s, e % 2, :], pack[e][:, a:b]).then_inc(w_in[s, part, e % 2], 16)

                    def thread(s):
                        sp.dma_start(xs[:, s], x[turn * THREADS + s].rearrange("(t p) d -> p t d", p=P))\
                            .then_inc(x_in[s], 16)
                        for st in NET:
                            steps = STEPS[st]
                            if st in ("X1", "X3"):
                                prev = {"X1": "X0", "X3": "X2"}[st]
                                sp.wait_ge(*after("scores", s, prev, ATT[prev] // H8 * TILES - 1))
                                sp.dma_start(kb[:, s, 0:ATT[st] * KEYS], keys_dram[st][turn * THREADS + s])\
                                    .then_inc(keys_in[s], 16)
                            if st in EXPERTS:
                                n, pack = EXPERTS[st], {"F0": experts0, "F1": experts1}[st]
                                if st == "F1":
                                    sp.wait_ge(*after("gated", s, "F0", E0 - 1))
                                for e in range(2):
                                    load(s, 1, w1s, pack, e, 0, W1_COLS)
                                    load(s, 2, w2s, pack, e, W1_COLS, EXPERT_COLS)
                                if st == "F1":
                                    for k in range(steps - n - 5):
                                        yield
                                    for i in range(n + 3):
                                        if 1 <= i and i + 1 < n:
                                            sp.wait_ge(*after("hidden in", s, st, i - 1))
                                            load(s, 1, w1s, pack, i + 1, 0, W1_COLS)
                                        if 2 <= i < n:
                                            sp.wait_ge(*after("expert out", s, st, i - 2))
                                            load(s, 2, w2s, pack, i, W1_COLS, EXPERT_COLS)
                                        yield
                                else:
                                    for k in range(steps - n - 3):
                                        yield
                                    for e in range(n + 1):
                                        if e and e + 1 < n:
                                            sp.wait_ge(*after("gated", s, st, e - 1))
                                            load(s, 2, w2s, pack, e + 1, W1_COLS, EXPERT_COLS)
                                        if e + 2 < n:
                                            sp.wait_ge(*after("hidden", s, st, e, FT - 1))
                                            load(s, 1, w1s, pack, e + 2, 0, W1_COLS)
                                        yield
                                yield
                                yield
                            else:
                                for k in range(steps):
                                    if st == "F3" and k == steps - 1:
                                        sp.wait_ge(*after("x done", s, "F3"))
                                        sp.dma_start(out[turn * THREADS + s].rearrange("(t p) d -> p t d", p=P),
                                                     xs[:, s]).then_inc(x_out[s], 16)
                                    yield

                    merged(thread)
                    for s in range(THREADS):
                        sp.wait_ge(x_out[s], 16)

                @block.tensor
                def _(pe):
                    t = Progress("pe", plan)
                    last = {}

                    def claim(s, banks, *key):
                        for b in banks:
                            if (s, b) in last:
                                pe.wait_ge(*after("read", s, b, *last[s, b]))
                            last[s, b] = key

                    def turned(st, s):
                        claim(s, "t", st, "xn")
                        pe.wait_ge(*after("xn", s, st))
                        for k in range(TILES):
                            ins = nc.tensor.transpose(tb[:, s, k * P:(k + 1) * P], xn[:, s, k, :], ident[:, :])
                        ins.then_inc(*t.tick("in t", s, st, "xn"))

                    def turned_back(st, s, *part):
                        claim(s, "t", st, "y")
                        pe.wait_ge(*after("yT", s, st, *part))
                        for k in range(TILES):
                            ins = nc.tensor.transpose(tb[:, s, k * P:(k + 1) * P], yT[:, s, k * P:(k + 1) * P],
                                                      ident[:, :])
                        ins.then_inc(*t.tick("in t", s, st, "y"))

                    def attention(st, s):
                        heads = ATT[st]
                        units = heads // H8 * TILES
                        pe.wait_ge(*after("ctx cols", s, st))
                        for n in range(heads // 4):
                            b = "ty"[n % 2]
                            claim(s, b, st, "v", n)
                            nc.tensor.matmul((tb, yb)[n % 2][0:KEYS, s, :], ctxb[:, s, :],
                                             C[st][:, n * 512:(n + 1) * 512], start=True, stop=True)\
                                .then_inc(*t.tick("v", s, st, n))
                        for k in range(NORM_STEPS[st]):
                            yield
                        yield
                        turned(st, s)
                        yield
                        pe.wait_ge(*after("xnT", s, st))
                        query = xnT
                        if st in HEADROWS:
                            query = qT
                            claim(s, "y", st, "q")
                            nc.tensor.matmul(yb[:, s, :], small_("wq0" if st == "X0" else "wq2"), xnT[:, s, :],
                                             start=True, stop=True).then_inc(*t.tick("q", s, st))
                        yield
                        if st in HEADROWS:
                            pe.wait_ge(*after("qT", s, st))
                            pe.wait_ge(*after("keys", s, st))
                        else:
                            pe.wait_ge(keys_in[s], 16 if st == "X1" else 32)

                        def scores(u):
                            hf, k = u // TILES, u % TILES
                            claim(s, "ab", st, u)
                            for j in range(2):
                                c = (hf * H8 + 4 * j) * KEYS
                                ins = nc.tensor.matmul(sc[:, s, j, 0:4 * KEYS], query[:, s, k * P:(k + 1) * P],
                                                       kb[:, s, c:c + 4 * KEYS], start=True, stop=True)
                            ins.then_inc(*t.tick("scores", s, st, u))

                        def turn_probs(u, j):
                            if j == 0:
                                pe.wait_ge(*after("probs", s, st, u))
                            claim(s, "t", st, u, j)
                            for i in range(4):
                                ins = nc.tensor.transpose(tb[0:KEYS, s, i * P:(i + 1) * P],
                                                          unit(s, u)[:, (4 * j + i) * KEYS:(4 * j + i + 1) * KEYS],
                                                          ident[:, :])
                            ins.then_inc(*t.tick("turned probs", s, st, u, j))

                        def values(u, part):
                            hf, q = u // TILES, u % TILES * P
                            if u == part == 0:
                                claim(s, "y", st, "y")
                                nc.tensor.matmul(yb[:, s, :], sel[64:65, 0, :], sel[64:65, 0:SEQ // P, :],
                                                 start=True, stop=False)
                            if part == 0:
                                pe.wait_ge(*after("read", s, "t", st, u + 1, 1))
                            for h in range(4 * part, 4 * part + 4):
                                g = hf * H8 + h
                                ins = nc.tensor.matmul(yb[:, s, q:q + 2 * P], vp[0:KEYS, s, g * D:(g + 1) * D],
                                                       big[0:KEYS, s, h * SEQ + q:h * SEQ + q + 2 * P],
                                                       start=False, stop=(u == units - 2 and g == heads - 1))
                            ins.then_inc(*t.tick("values", s, st, u))

                        for k in range(units + 2):
                            if k >= 2:
                                turn_probs(k - 2, 0)
                            if k < units:
                                scores(k)
                            if st == "X2":
                                yield
                            if k >= 4:
                                values((k - 4) // 2 * 2, k % 2)
                            if k >= 2:
                                turn_probs(k - 2, 1)
                            for _ in range(max(1, SUBSTEPS[st] - 1)):
                                yield
                        values(units - 2, 0)
                        values(units - 2, 1)
                        plan.labels[("y done", s, st)] = ("pe", t.count)
                        yield
                        turned_back(st, s)
                        yield

                    def routed(st, s):
                        n = EXPERTS[st]
                        for k in range(TOPK_STEPS):
                            yield
                        claim(s, "t", st, "taken")
                        pe.wait_ge(*after("takenT", s))
                        for k in range(TILES):
                            ins = nc.tensor.transpose(tb[:, s, k * E1:(k + 1) * E1], prT[s][:, k * P:(k + 1) * P],
                                                      ident[0:E1, 0:E1])
                        ins.then_inc(*t.tick("taken in", s))
                        claim(s, "y", st, "slots")
                        pe.wait_ge(*after("taken", s))
                        for k in range(TILES):
                            for j in range(k + 1):
                                ins = nc.tensor.matmul(yb[:, s, k * E1:(k + 1) * E1],
                                                       (upto if j == k else onesb)[:, :], taken[:, s, j, :],
                                                       start=(j == 0), stop=(j == k))
                        ins.then_inc(*t.tick("slots in", s))
                        yield

                        def gather(e):
                            claim(s, "b", st, "xg", e)
                            pe.wait_ge(*after("hot", s, e))
                            for k in range(TILES):
                                ins = nc.tensor.matmul(sc[:, s, 1, 0:P], xn[:, s, k, :], hot[s][:, e % 2, k, :],
                                                       start=(k == 0), stop=(k == TILES - 1))
                            ins.then_inc(*t.tick("gathered", s, e))

                        def hidden(e):
                            claim(s, "a", st, e)
                            pe.wait_ge(w_in[s, 1, e % 2], 16 * (e // 2 + 1 + E0 // 2))
                            pe.wait_ge(*after("read", s, "b", st, "xg", e))
                            for f in range(FT):
                                ins = nc.tensor.matmul(sc[:, s, 0, f * P:(f + 1) * P],
                                                       w1s[:, s, e % 2, f * P:(f + 1) * P], xg[s][:, e % 2, :],
                                                       start=True, stop=True)
                            ins.then_inc(*t.tick("hidden in", s, st, e))

                        def turn_hot(e):
                            claim(s, "t", st, "hot", e)
                            pe.wait_ge(*after("hot gated", s, e))
                            for k in range(TILES):
                                ins = nc.tensor.transpose(tb[:, s, k * P:(k + 1) * P], hotg[s][:, e % 2, k, :],
                                                          ident[:, :])
                            ins.then_inc(*t.tick("hot turned", s, e))

                        def result(e):
                            claim(s, "b", st, "og", e)
                            pe.wait_ge(w_in[s, 2, e % 2], 16 * (e // 2 + 1 + E0 // 2))
                            pe.wait_ge(*after("read", s, "a", st, e))
                            for f in range(FT):
                                g = (e % 2) * FT * P + f * P
                                ins = nc.tensor.matmul(sc[:, s, 1, 0:P], big[:, s, g:g + P],
                                                       w2s[:, s, e % 2, f * P:(f + 1) * P],
                                                       start=(f == 0), stop=(f == FT - 1))
                            ins.then_inc(*t.tick("expert out", s, st, e))

                        def scatter(e):
                            if e == 0:
                                claim(s, "y", st, "y")
                            pe.wait_ge(*after("read", s, "b", st, "og", e))
                            pe.wait_ge(*after("read", s, "t", st, "hot", e))
                            nc.tensor.matmul(yb[:, s, :], og[s][:, e % 2, :], hotT[s][:, e % 2, :],
                                             start=(e == 0), stop=(e == n - 1)).then_inc(*t.tick("y done", s, st))

                        for i in range(n + 3):
                            if i < n:
                                gather(i)
                            if 1 <= i <= n:
                                hidden(i - 1)
                            if 2 <= i <= n + 1:
                                turn_hot(i - 2)
                                result(i - 2)
                            if i >= 3:
                                scatter(i - 3)
                            yield
                        turned_back(st, s)
                        yield
                        yield

                    def experts(st, s):
                        n = EXPERTS[st]
                        for k in range(NORM_STEPS[st]):
                            yield
                        yield
                        turned(st, s)
                        yield
                        pe.wait_ge(*after("xnT", s, st))
                        claim(s, "y", st, "logits")
                        for k in range(TILES):
                            tile = xnT[:, s, k * P:(k + 1) * P]
                            if st == "F0":
                                nc.tensor.matmul(yb[:, s, k * E0:(k + 1) * E0], tile, R0[:, :], start=True, stop=False)
                                ins = nc.tensor.matmul(yb[:, s, k * E0:(k + 1) * E0], ones[0:1, :], c0row[:, :],
                                                       start=False, stop=True)
                            else:
                                ins = nc.tensor.matmul(yb[:, s, k * E1:(k + 1) * E1], tile, small_("gwT"),
                                                       start=True, stop=True)
                        ins.then_inc(*t.tick("logits", s, st))

                        def hidden(e, part):
                            if part == 0:
                                pe.wait_ge(w_in[s, 1, e % 2], 16 * (e // 2 + 1))
                            for f in (2 * part, 2 * part + 1):
                                claim(s, "ab"[f % 2], st, e, f)
                                nc.tensor.matmul(sc[:, s, f % 2, :], w1s[:, s, e % 2, f * P:(f + 1) * P],
                                                 xnT[:, s, :], start=True, stop=True)\
                                    .then_inc(*t.tick("hidden in", s, st, e, f))

                        if st == "F0":
                            hidden(0, 0)
                        yield
                        if st == "F0":
                            hidden(0, 1)
                        claim(s, "y", st, "gates")
                        if st == "F0":
                            ybb = yb[:, s, :].bitcast(BF16)
                            pe.wait_ge(*after("gate parts", s))
                            for k in range(TILES):
                                ins = nc.tensor.transpose(ybb[:, k * P:(k + 1) * P], c3[:, s, k, :], identb[:, :])
                        else:
                            pe.wait_ge(*after("expert probs", s, st))
                            for k in range(TILES):
                                ins = nc.tensor.transpose(yb[0:E1, s, k * P:(k + 1) * P], pr[:, s, k, :], ident[:, :])
                        ins.then_inc(*t.tick("gates turned", s, st))
                        yield
                        if st == "F1":
                            yield from routed(st, s)
                            return

                        def result(e):
                            claim(s, "t", st, e)
                            pe.wait_ge(w_in[s, 2, e % 2], 16 * (e // 2 + 1))
                            for f in range(FT):
                                pe.wait_ge(*after("hidden", s, st, e, f))
                                ins = nc.tensor.matmul(tb[:, s, :], w2s[:, s, e % 2, f * P:(f + 1) * P],
                                                       big[:, s, ((e % 2) * FT + f) * SEQ:((e % 2) * FT + f + 1) * SEQ],
                                                       start=(f == 0), stop=(f == FT - 1))
                            ins.then_inc(*t.tick("expert out", s, st, e))

                        for e in range(n + 1):
                            if e + 1 < n:
                                hidden(e + 1, 0)
                            if e < n:
                                result(e)
                            if e + 1 < n:
                                hidden(e + 1, 1)
                            if e < n:
                                if e == 0:
                                    pe.wait_ge(*after("read", s, "y", st, "gates"))
                                claim(s, "y", st, "row", e)
                                nc.tensor.matmul(yb[:, s, :], sel[:, e, :], c3T[:, s, :], start=True, stop=True)\
                                    .then_inc(*t.tick("gate row in", s, st, e))
                            yield
                        turned_back(st, s, n - 1)
                        yield
                        yield

                    def self_attention(st, s):
                        for k in range(NORM_STEPS[st]):
                            yield
                        yield
                        turned(st, s)
                        yield
                        pe.wait_ge(*after("xnT", s, st))
                        claim(s, "y", st, "gate")
                        for k in range(TILES):
                            ins = nc.tensor.matmul(yb[:, s, k * H8:(k + 1) * H8], xnT[:, s, k * P:(k + 1) * P],
                                                   small_("wsT"), start=True, stop=True)
                        ins.then_inc(*t.tick("gate in", s))

                        def value_tiles(g, tiles):
                            for k in tiles:
                                b, bank = value_bank(s, g, k)
                                claim(s, b, st, "v", g, k)
                                nc.tensor.matmul(bank, xnT[:, s, k * P:(k + 1) * P],
                                                 CF[:, g * 512:(g + 1) * 512], start=True, stop=True)\
                                    .then_inc(*t.tick("vF", s, g, k))

                        def keys(h):
                            claim(s, "t", st, "k", h)
                            nc.tensor.matmul(tb[:, s, :], AF[:, h * P:(h + 1) * P], xnT[:, s, :], start=True, stop=True)\
                                .then_inc(*t.tick("kF", s, h))

                        def scores(k):
                            h, r = k // 2, k % 2
                            claim(s, "ab", st, k)
                            pe.wait_ge(*after("read", s, "t", st, "k", h))
                            for i in range(2):
                                q = 2 * r + i
                                ins = nc.tensor.matmul(sc[:, s, i, :], xnT[:, s, q * P:(q + 1) * P], kpt[:, s, h % 2, :],
                                                       start=True, stop=True)
                            ins.then_inc(*t.tick("scoresF", s, k))

                        def turn_probs(k, i):
                            if i == 0:
                                pe.wait_ge(*after("probs", s, st, k))
                            claim(s, "t", st, k, i)
                            for q in range(TILES):
                                c = (k % 2) * 2 * SEQ + i * SEQ + q * P
                                ins = nc.tensor.transpose(tb[:, s, q * P:(q + 1) * P], ee[:, s, c:c + P], ident[:, :])
                            ins.then_inc(*t.tick("turned probs", s, st, k, i))

                        def values(h, part):
                            if part == 0:
                                for i in range(2):
                                    pe.wait_ge(*after("read", s, "t", st, 2 * h + 1, i))
                                pe.wait_ge(*after("read", s, value_bank(s, h // 4, TILES - 1)[0], st, "v", h // 4,
                                                  TILES - 1))
                            for k in range(2 * part, 2 * part + 2):
                                c = k * 512 + (h % 4) * D
                                g = (h % 2) * TILES + k
                                ins = nc.tensor.matmul(yb[:, s, :], vp[:, s, c:c + D], big[:, s, g * SEQ:(g + 1) * SEQ],
                                                       start=False, stop=(h == H8 - 1 and k == TILES - 1))
                            ins.then_inc(*t.tick("valuesF", s, h))

                        value_tiles(0, range(TILES))
                        keys(0)
                        yield
                        claim(s, "t", st, "gatesT")
                        pe.wait_ge(*after("gates", s))
                        for k in range(TILES):
                            ins = nc.tensor.transpose(tb[0:H8, s, k * P:(k + 1) * P], gt[:, s, k, :], ident[:, :])
                        ins.then_inc(*t.tick("gatesT in", s))
                        claim(s, "y", st, "y")
                        pe.wait_ge(*after("read", s, "t", st, "gatesT"))
                        nc.tensor.matmul(yb[:, s, :], boF[:, :], gtT[:, s, :], start=True, stop=False)
                        yield
                        for k in range(2 * H8 + 2):
                            if k >= 2:
                                turn_probs(k - 2, 0)
                            if k < 2 * H8:
                                scores(k)
                            if k >= 4:
                                values((k - 4) // 2, k % 2)
                            if k >= 2:
                                turn_probs(k - 2, 1)
                            if k % 2 and (k + 1) // 2 < H8:
                                keys((k + 1) // 2)
                            if k in (10, 11):
                                value_tiles(1, range(2 * (k - 10), 2 * (k - 10) + 2))
                            yield
                        values(H8 - 1, 0)
                        values(H8 - 1, 1)
                        plan.labels[("y done", s, st)] = ("pe", t.count)
                        yield
                        turned_back(st, s)
                        yield

                    def ternary(st, s):
                        for k in range(NORM_STEPS[st]):
                            yield
                        yield
                        turned(st, s)
                        yield
                        pe.wait_ge(*after("xnT", s, st))
                        for f in range(FT):
                            claim(s, "ab"[f % 2], st, f)
                            nc.tensor.matmul(sc[:, s, f % 2, :], W1q[:, f * P:(f + 1) * P], xnT[:, s, :],
                                             start=True, stop=True).then_inc(*t.tick("hidden3 in", s, f))
                        yield
                        claim(s, "y", st, "y")
                        for f in range(FT):
                            pe.wait_ge(*after("read", s, "ab"[f % 2], st, f))
                            ins = nc.tensor.matmul(yb[:, s, :], W2q[:, f * P:(f + 1) * P],
                                                   big[:, s, f * SEQ:(f + 1) * SEQ], start=(f == 0), stop=(f == FT - 1))
                        ins.then_inc(*t.tick("y done", s, st))
                        yield
                        turned_back(st, s)
                        yield

                    merged(lambda s: network_of(s, attention, experts, self_attention, ternary))
                    pe.wait_ge(*t.now())

                @block.scalar
                def _(act):
                    a = Progress("act", plan)

                    def read(s, banks, *key):
                        for b in banks:
                            plan.labels[("read", s, b) + key] = ("act", a.count)

                    def turned(st, s):
                        act.wait_ge(*after("in t", s, st, "xn"))
                        if st == "X1":
                            ins = nc.scalar.activation(xnT[:, s, :], tb[:, s, :], ACT.Identity, bias=vec("beta"),
                                                       scale=vec("gamma"))
                        else:
                            ins = nc.scalar.activation(xnT[:, s, :], tb[:, s, :], ACT.Copy)
                        ins.then_inc(*a.tick("xnT", s, st))
                        read(s, "t", st, "xn")

                    def result(st, s):
                        act.wait_ge(*after("y done", s, st))
                        if st == "X1":
                            ins = nc.scalar.activation(yT[:, s, :], yb[:, s, :], ACT.Identity, bias=bo1g[:, :],
                                                       scale=tg[:, :])
                        elif st in ("F1", "F2"):
                            ins = nc.scalar.activation(yT[:, s, :], yb[:, s, :], ACT.Copy)
                        else:
                            b = {"X0": "bo0", "X2": "bo2", "X3": "bo3", "F3": "b2_3"}[st]
                            ins = nc.scalar.activation(yT[:, s, :], yb[:, s, :], ACT.Identity, bias=vec(b))
                        ins.then_inc(*a.tick("yT", s, st))
                        read(s, "y", st, "y")

                    def attention(st, s):
                        heads = ATT[st]
                        units = heads // H8 * TILES
                        for n in range(heads // 4):
                            act.wait_ge(*after("v", s, st, n))
                            nc.scalar.activation(vp[0:KEYS, s, n * 512:(n + 1) * 512], (tb, yb)[n % 2][0:KEYS, s, :],
                                                 ACT.Copy).then_inc(*a.tick())
                            read(s, "ty"[n % 2], st, "v", n)
                        for k in range(NORM_STEPS[st]):
                            yield
                        yield
                        turned(st, s)
                        yield
                        if st in HEADROWS:
                            act.wait_ge(*after("q", s, st))
                            nc.scalar.activation(qT[:, s, :], yb[:, s, :], ACT.Identity,
                                                 bias=vec("bq0" if st == "X0" else "bq2")).then_inc(*a.tick("qT", s, st))
                            read(s, "y", st, "q")
                        yield
                        dst = big[:, s, :].rearrange("p (h q) -> p h q", h=H8)
                        for k in range(units + 2):
                            if k >= 2:
                                u = k - 2
                                for j in range(2):
                                    if j and st == "X2":
                                        yield
                                    act.wait_ge(*after("turned probs", s, st, u, j))
                                    nc.scalar.activation(
                                        dst[0:KEYS, 4 * j:4 * j + 4, (u % TILES) * P:(u % TILES + 1) * P],
                                        tb[0:KEYS, s, :].rearrange("p (h q) -> p h q", h=4), ACT.Copy)\
                                        .then_inc(*a.tick())
                                    read(s, "t", st, u, j)
                            elif st == "X2":
                                yield
                            if k < units and st == "X2":
                                act.wait_ge(*after("minus peak", s, st, k))
                                for h in range(H8):
                                    nc.scalar.activation(unit(s, k)[:, h * KEYS:(h + 1) * KEYS],
                                                         sc[:, s, h // 4, (h % 4) * KEYS:(h % 4 + 1) * KEYS], ACT.Exp,
                                                         bias=minus_peak[:, s, h:h + 1], scale=SCALE[st])\
                                        .then_inc(*a.tick("exps", s, st, k))
                                read(s, "ab", st, k)
                            elif k < units:
                                act.wait_ge(*after("shifted", s, st, k))
                                nc.scalar.activation(unit(s, k), unit(s, k), ACT.Exp, scale=SCALE[st])\
                                    .then_inc(*a.tick("exps", s, st, k))
                            for _ in range(max(1, SUBSTEPS[st] - 1)):
                                yield
                        result(st, s)
                        yield
                        yield

                    def routed(st, s):
                        n = EXPERTS[st]
                        for k in range(TOPK_STEPS + 1):
                            yield
                        for i in range(n + 3):
                            if i < n:
                                act.wait_ge(*after("gathered", s, i))
                                nc.scalar.activation(xg[s][:, i % 2, :], sc[:, s, 1, 0:P], ACT.Copy).then_inc(*a.tick())
                                read(s, "b", st, "xg", i)
                            if 1 <= i <= n:
                                e = i - 1
                                act.wait_ge(*after("hidden in", s, st, e))
                                c = (e % 2) * FT * P
                                nc.scalar.activation(big[:, s, c:c + FT * P], sc[:, s, 0, :], ACT.Gelu)\
                                    .then_inc(*a.tick())
                                read(s, "a", st, e)
                            if 2 <= i <= n + 1:
                                e = i - 2
                                act.wait_ge(*after("hot turned", s, e))
                                nc.scalar.activation(hotT[s][:, e % 2, :], tb[:, s, :], ACT.Copy).then_inc(*a.tick())
                                read(s, "t", st, "hot", e)
                                act.wait_ge(*after("expert out", s, st, e))
                                nc.scalar.activation(og[s][:, e % 2, :], sc[:, s, 1, 0:P], ACT.Copy)\
                                    .then_inc(*a.tick())
                                read(s, "b", st, "og", e)
                            yield
                        result(st, s)
                        yield
                        yield

                    def experts(st, s):
                        n = EXPERTS[st]
                        for k in range(NORM_STEPS[st]):
                            yield
                        if st == "F0":
                            act.wait_ge(*after("xn", s, st))
                            for k in range(TILES):
                                nc.scalar.activation(tmp[:, s, k * D:(k + 1) * D], xn[:, s, k, :], ACT.Square,
                                                     accum_out=sq[:, s, k:k + 1]).then_inc(*a.tick("norms", s))
                        yield
                        turned(st, s)
                        yield
                        act.wait_ge(*after("router shifted", s, st))
                        nc.scalar.activation(ex[:, s, :, 0:n], ex[:, s, :, 0:n], ACT.Exp)\
                            .then_inc(*a.tick("router exps", s, st))

                        def hidden(e, part):
                            for f in (2 * part, 2 * part + 1):
                                act.wait_ge(*after("hidden in", s, st, e, f))
                                g = (e % 2) * FT + f
                                nc.scalar.activation(big[:, s, g * SEQ:(g + 1) * SEQ], sc[:, s, f % 2, :], ACT.Gelu,
                                                     bias=w1s[:, s, e % 2, FT * P + f:FT * P + f + 1])\
                                    .then_inc(*a.tick("hidden", s, st, e, f))
                                read(s, "ab"[f % 2], st, e, f)

                        if st == "F0":
                            hidden(0, 0)
                        yield
                        if st == "F0":
                            hidden(0, 1)
                        act.wait_ge(*after("gates turned", s, st))
                        if st == "F0":
                            nc.scalar.activation(c3T[:, s, :], yb[:, s, :].bitcast(BF16)[:, 0:SEQ], ACT.Copy)\
                                .then_inc(*a.tick())
                        else:
                            nc.scalar.activation(prT[s], yb[0:E1, s, :], ACT.Copy).then_inc(*a.tick("prT", s))
                        read(s, "y", st, "gates")
                        yield
                        if st == "F1":
                            yield from routed(st, s)
                            return
                        for e in range(n + 1):
                            if e + 1 < n:
                                hidden(e + 1, 0)
                                hidden(e + 1, 1)
                            if e < n:
                                act.wait_ge(*after("gate row in", s, st, e))
                                if e:
                                    act.wait_ge(*after("gated", s, st, e - 1))
                                nc.scalar.activation(cb[:, s, :], yb[:, s, :], ACT.Copy)\
                                    .then_inc(*a.tick("gate row", s, st, e))
                                read(s, "y", st, "row", e)
                            yield
                        yield
                        yield

                    def self_attention(st, s):
                        for k in range(NORM_STEPS[st]):
                            yield
                        yield
                        turned(st, s)
                        yield
                        act.wait_ge(*after("gate in", s))
                        nc.scalar.activation(sg[:, s, :, 0:H8],
                                             yb[:, s, 0:TILES * H8].rearrange("p (t h) -> p t h", h=H8),
                                             ACT.Exp, scale=-1.0).then_inc(*a.tick("exp gates", s))
                        read(s, "y", st, "gate")

                        def keys(h):
                            act.wait_ge(*after("kF", s, h))
                            nc.scalar.activation(kpt[:, s, h % 2, :], tb[:, s, :], ACT.Copy).then_inc(*a.tick())
                            read(s, "t", st, "k", h)

                        def value_tiles(g, tiles):
                            for k in tiles:
                                b, bank = value_bank(s, g, k)
                                act.wait_ge(*after("vF", s, g, k))
                                nc.scalar.activation(vp[:, s, k * 512:(k + 1) * 512], bank, ACT.Copy)\
                                    .then_inc(*a.tick())
                                read(s, b, st, "v", g, k)

                        value_tiles(0, range(TILES))
                        keys(0)
                        yield
                        act.wait_ge(*after("gatesT in", s))
                        nc.scalar.activation(gtT[:, s, :], tb[0:H8, s, :], ACT.Copy).then_inc(*a.tick())
                        read(s, "t", st, "gatesT")
                        yield
                        for k in range(2 * H8 + 2):
                            if k >= 2:
                                h, r = (k - 2) // 2, k % 2
                                dst = big[:, s, (h % 2) * TILES * SEQ:(h % 2 + 1) * TILES * SEQ]\
                                    .rearrange("p (k q) -> p k q", k=TILES)
                                act.wait_ge(*after("turned probs", s, st, k - 2, 0))
                                nc.scalar.activation(dst[:, :, 2 * r * P:(2 * r + 1) * P],
                                                     tb[:, s, :].rearrange("p (k q) -> p k q", k=TILES), ACT.Copy)\
                                    .then_inc(*a.tick())
                                read(s, "t", st, k - 2, 0)
                            if k < 2 * H8:
                                act.wait_ge(*after("maxima", s, k))
                                if k >= 2:
                                    act.wait_ge(*after("turned probs", s, st, k - 2, 1))
                                for i in range(2):
                                    c = (k % 2) * 2 * SEQ + i * SEQ
                                    nc.scalar.activation(ee[:, s, c:c + SEQ], sc[:, s, i, :], ACT.Exp,
                                                         bias=mx[:, s, k % 2, i:i + 1],
                                                         accum_out=dn[:, s, k % 2, i:i + 1])\
                                        .then_inc(*a.tick("exps", s, st, k))
                                read(s, "ab", st, k)
                            if k % 2 and (k + 1) // 2 < H8:
                                keys((k + 1) // 2)
                            if k in (10, 11):
                                value_tiles(1, range(2 * (k - 10), 2 * (k - 10) + 2))
                            yield
                        result(st, s)
                        yield
                        yield

                    def ternary(st, s):
                        for k in range(NORM_STEPS[st]):
                            yield
                        yield
                        turned(st, s)
                        yield
                        for f in range(FT):
                            act.wait_ge(*after("hidden3 in", s, f))
                            nc.scalar.activation(big[:, s, f * SEQ:(f + 1) * SEQ], sc[:, s, f % 2, :], ACT.Relu,
                                                 bias=vec("b1_3a", FT)[:, f:f + 1]).then_inc(*a.tick())
                            read(s, "ab"[f % 2], st, f)
                        yield
                        result(st, s)
                        yield
                        yield

                    merged(lambda s: network_of(s, attention, experts, self_attention, ternary))
                    act.wait_ge(*a.now())

                @block.vector
                def _(dve):
                    v = Progress("dve", plan)

                    def read(s, banks, *key):
                        for b in banks:
                            plan.labels[("read", s, b) + key] = ("dve", v.count)

                    def norm(st, s):
                        src = xs
                        for again in range(NORM_STEPS[st]):
                            dve.wait_ge(*v.now())
                            for k in range(TILES):
                                nc.vector.bn_stats(stats[:, s, k, :], src[:, s, k, :]).then_inc(*v.tick())
                            dve.wait_ge(*v.now())
                            for k in range(TILES):
                                nc.vector.bn_aggr(mv[:, s, k, :], stats[:, s, k, :]).then_inc(*v.tick())
                            dve.wait_ge(*v.now())
                            nc.vector.tensor_scalar(ve[:, s, :], mv[:, s, :, 1], EPS, None, ALU.add)\
                                .then_inc(*v.tick("variance", s, st, again))
                            yield
                            dve.wait_ge(*after("rstd", s, st, again))
                            for k in range(TILES):
                                nc.vector.tensor_scalar(xn[:, s, k, :], src[:, s, k, :], mv[:, s, k, 0:1],
                                                        rstd[:, s, k:k + 1], ALU.subtract, ALU.mult)\
                                    .then_inc(*v.tick("xn", s, st))
                            src = xn

                    def residual(st, s):
                        dve.wait_ge(*after("in t", s, st, "y"))
                        flat = xs[:, s].rearrange("p t d -> p (t d)")
                        nc.vector.tensor_tensor(flat, flat, tb[:, s, :], ALU.add).then_inc(*v.tick("x done", s, st))
                        read(s, "t", st, "y")

                    def attention(st, s):
                        yield from norm(st, s)
                        yield
                        yield
                        yield
                        units = ATT[st] // H8 * TILES

                        def topk_round(u, rnd):
                            dve.wait_ge(*after("scores", s, st, u))
                            m8 = m8b if rnd else m8a
                            for kind in ("max", "replace"):
                                base = topk_round.base if kind == "max" else v.count - H8
                                for h in range(H8):
                                    work = wk[:, s, u % 2, h * KEYS:(h + 1) * KEYS]
                                    src = work if rnd else sc[:, s, h // 4, (h % 4) * KEYS:(h % 4 + 1) * KEYS]
                                    if rnd or kind == "replace":
                                        dve.wait_ge(sems["dve"], base + h + 1)
                                    if kind == "max":
                                        nc.vector.max(m8[:, s, h, :], src).then_inc(*v.tick())
                                    else:
                                        nc.vector.match_replace(work, m8[:, s, h, :], src, TAKEN).then_inc(*v.tick())
                            topk_round.base = v.count - H8
                            if rnd == 0:
                                dve.wait_ge(*v.now())
                                nc.vector.tensor_scalar(minus_peak[:, s, :], m8a[:, s, :, 0], -SCALE[st], None, ALU.mult)\
                                    .then_inc(*v.tick("minus peak", s, st, u))
                            if rnd == TOP2 // 8 - 1:
                                plan.labels[("top taken", s, st, u)] = ("dve", v.count)

                        topk_round.base = 0

                        def shift(u):
                            p = u % 2
                            scv = sc[:, s, :, 0:4 * KEYS].rearrange("p j (h k) -> p j h k", h=4)
                            dve.wait_ge(*after("scores", s, st, u))
                            nc.vector.tensor_reduce(mx[:, s, p, :].rearrange("p (j h) -> p j h", j=2), scv, AX.X,
                                                    ALU.max).then_inc(*v.tick())
                            dve.wait_ge(*v.now())
                            if u >= 3:
                                dve.wait_ge(*after("turned probs", s, st, u - 3, 1))
                            nc.vector.tensor_tensor(
                                unit(s, u).rearrange("p (j h k) -> p j h k", j=2, h=4), scv,
                                mx[:, s, p, :].rearrange("p (j h) -> p j h", j=2).unsqueeze(3).to_broadcast([P, 2, 4, KEYS]),
                                ALU.subtract).then_inc(*v.tick("shifted", s, st, u))
                            read(s, "ab", st, u)

                        def total(u):
                            p = u % 2
                            dve.wait_ge(*after("masked" if st == "X2" else "exps", s, st, u))
                            nc.vector.tensor_reduce(sums[:, s, p, :], unit(s, u).rearrange("p (h k) -> p h k", h=H8),
                                                    AX.X, ALU.add).then_inc(*v.tick())
                            dve.wait_ge(*v.now())
                            nc.vector.reciprocal(rs[:, s, p, :], sums[:, s, p, :]).then_inc(*v.tick("rsum", s, st, u))

                        for k in range(units + 2):
                            if st == "X2":
                                for rnd in range(TOP2 // 8):
                                    if rnd == 1 and 1 <= k <= units:
                                        total(k - 1)
                                    if k < units:
                                        topk_round(k, rnd)
                                    yield
                            else:
                                if 1 <= k <= units:
                                    total(k - 1)
                                if k < units:
                                    shift(k)
                                yield
                        yield
                        residual(st, s)
                        yield

                    def split(dsts, src, label):
                        for k, d in enumerate(dsts):
                            dve.wait_ge(*v.now())
                            nc.vector.tensor_copy(d, src).then_inc(*v.tick(*(label if k == 2 else ())))
                            if k < 2:
                                dve.wait_ge(*v.now())
                                nc.vector.tensor_tensor(src, src, d, ALU.subtract).then_inc(*v.tick())

                    def routed(st, s):
                        n = EXPERTS[st]
                        for rnd in range(TOP1 // 8):
                            if rnd == 0:
                                dve.wait_ge(*after("prT", s))
                            src = wkT[s] if rnd else prT[s]
                            dve.wait_ge(*v.now())
                            nc.vector.max(m16[:, s, :], src).then_inc(*v.tick())
                            dve.wait_ge(*v.now())
                            nc.vector.match_replace(wkT[s], m16[:, s, :], src, TAKEN).then_inc(*v.tick())
                            if rnd % 2:
                                yield
                        dve.wait_ge(*v.now())
                        nc.vector.tensor_scalar(prT[s], wkT[s], TAKEN_BELOW, None, ALU.is_le)\
                            .then_inc(*v.tick("takenT", s))
                        flat = lambda m: m[:, s, :, :].rearrange("p t e -> p (t e)")
                        dve.wait_ge(*after("taken in", s))
                        nc.vector.tensor_copy(flat(taken), tb[:, s, 0:TILES * E1]).then_inc(*v.tick("taken", s))
                        read(s, "t", st, "taken")
                        dve.wait_ge(*after("slots in", s))
                        nc.vector.tensor_tensor(flat(slot), yb[:, s, 0:TILES * E1], flat(taken), ALU.mult)\
                            .then_inc(*v.tick("slot", s))
                        read(s, "y", st, "slots")

                        def one_hot(e):
                            dve.wait_ge(*after("slot", s))
                            if e >= 2:
                                dve.wait_ge(*after("gathered", s, e - 2))
                                dve.wait_ge(*after("hot gated", s, e - 2))
                            nc.vector.tensor_tensor(hot[s][:, e % 2, :, :],
                                                    place[:, :].unsqueeze(1).to_broadcast([P, TILES, P]),
                                                    slot[:, s, :, e:e + 1].to_broadcast([P, TILES, P]), ALU.is_equal)\
                                .then_inc(*v.tick("hot", s, e))

                        one_hot(0)
                        yield
                        for i in range(n + 3):
                            if i + 1 < n:
                                one_hot(i + 1)
                            yield
                        residual(st, s)
                        yield
                        yield

                    def experts(st, s):
                        n = EXPERTS[st]
                        yield from norm(st, s)
                        yield
                        yield
                        dve.wait_ge(*after("logits", s, st))
                        logits = yb[:, s, 0:TILES * n].rearrange("p (t e) -> p t e", t=TILES)
                        e = ex[:, s, :, 0:n]
                        if st == "F0":
                            dve.wait_ge(*after("norms", s))
                            nc.vector.tensor_tensor(lg[:, s, :, 0:E0], logits,
                                                    sq[:, s, :].unsqueeze(2).to_broadcast([P, TILES, E0]),
                                                    ALU.subtract).then_inc(*v.tick())
                            read(s, "y", st, "logits")
                            dve.wait_ge(*v.now())
                            for k in range(TILES):
                                nc.vector.max(m8r[:, s, k, :], lg[:, s, k, 0:E0]).then_inc(*v.tick())
                            dve.wait_ge(*v.now())
                            nc.vector.tensor_copy(top[:, s, :, 0:TOP0], m8r[:, s, :, 0:TOP0]).then_inc(*v.tick())
                            nc.vector.tensor_tensor(e, lg[:, s, :, 0:E0], m8r[:, s, :, 0:1].to_broadcast([P, TILES, E0]),
                                                    ALU.subtract).then_inc(*v.tick("router shifted", s, st))
                            dve.wait_ge(*v.now())
                            for k in range(TILES):
                                nc.vector.match_replace(lgw[:, s, k, :], top[:, s, k, :], lg[:, s, k, :], TAKEN)\
                                    .then_inc(*v.tick())
                        else:
                            nc.vector.tensor_reduce(den[:, s, :], logits, AX.X, ALU.max).then_inc(*v.tick())
                            dve.wait_ge(*v.now())
                            nc.vector.tensor_tensor(e, logits, den[:, s, :].unsqueeze(2).to_broadcast([P, TILES, E1]),
                                                    ALU.subtract).then_inc(*v.tick("router shifted", s, st))
                            read(s, "y", st, "logits")
                        yield
                        dve.wait_ge(*after("router exps", s, st))
                        dve.wait_ge(*v.now())
                        if st == "F0":
                            nc.vector.scalar_tensor_tensor(e, lgw[:, s, :, 0:E0], TAKEN_BELOW, e, ALU.is_le, ALU.mult)\
                                .then_inc(*v.tick())
                            dve.wait_ge(*v.now())
                        nc.vector.tensor_reduce(den[:, s, :], e, AX.X, ALU.add).then_inc(*v.tick())
                        dve.wait_ge(*v.now())
                        nc.vector.reciprocal(rden[:, s, :], den[:, s, :]).then_inc(*v.tick())
                        dve.wait_ge(*v.now())
                        dst = cw[:, s, :, :] if st == "F0" else pr[:, s, :, :]
                        nc.vector.tensor_tensor(dst, e, rden[:, s, :].unsqueeze(2).to_broadcast([P, TILES, n]),
                                                ALU.mult).then_inc(*v.tick("expert probs", s, st))
                        if st == "F0":
                            split([c3[:, s, :, k * E0:(k + 1) * E0] for k in range(3)], cw[:, s, :, :],
                                  ("gate parts", s))
                            nc.vector.memset(yT[:, s, :], 0.0).then_inc(*v.tick("yT", s, st, -1))
                        yield
                        if st == "F1":
                            yield from routed(st, s)
                            return
                        for i in range(n + 1):
                            if i:
                                dve.wait_ge(*after("gate row", s, st, i - 1))
                                dve.wait_ge(*after("expert out", s, st, i - 1))
                                dve.wait_ge(*after("yT", s, st, i - 2))
                                nc.vector.scalar_tensor_tensor(tmp[:, s, :], tb[:, s, :],
                                                               w2s[:, s, (i - 1) % 2, FT * P:FT * P + 1],
                                                               cb[:, s, :], ALU.add, ALU.mult)\
                                    .then_inc(*v.tick("gated", s, st, i - 1))
                                read(s, "t", st, i - 1)
                                dve.wait_ge(*v.now())
                                nc.vector.tensor_tensor(yT[:, s, :], yT[:, s, :], tmp[:, s, :], ALU.add)\
                                    .then_inc(*v.tick("yT", s, st, i - 1))
                            yield
                        residual(st, s)
                        yield
                        yield

                    def self_attention(st, s):
                        yield from norm(st, s)
                        yield
                        yield
                        yield
                        g = sg[:, s, :, 0:H8]
                        dve.wait_ge(*after("exp gates", s))
                        nc.vector.tensor_scalar(g, g, 1.0, None, ALU.add).then_inc(*v.tick())
                        dve.wait_ge(*v.now())
                        nc.vector.reciprocal(g, g).then_inc(*v.tick())
                        dve.wait_ge(*v.now())
                        for k in range(TILES):
                            nc.vector.max(m8r[:, s, k, :], sg[:, s, k, 0:H8]).then_inc(*v.tick())
                        dve.wait_ge(*v.now())
                        nc.vector.tensor_copy(topF[:, s, :, 0:TOPF2], m8r[:, s, :, 0:TOPF2]).then_inc(*v.tick())
                        dve.wait_ge(*v.now())
                        for k in range(TILES):
                            nc.vector.match_replace(sgw[:, s, k, :], topF[:, s, k, :], sg[:, s, k, :], TAKEN)\
                                .then_inc(*v.tick())
                        dve.wait_ge(*v.now())
                        nc.vector.scalar_tensor_tensor(gt[:, s, :, :], sgw[:, s, :, 0:H8], TAKEN_BELOW, g, ALU.is_le,
                                                       ALU.mult).then_inc(*v.tick("gates", s))
                        yield
                        for k in range(2 * H8 + 2):
                            if 1 <= k <= 2 * H8:
                                p, h, r = (k - 1) % 2, (k - 1) // 2, (k - 1) % 2
                                dve.wait_ge(*after("exps", s, st, k - 1))
                                nc.vector.reciprocal(rg[:, s, p, :], dn[:, s, p, :]).then_inc(*v.tick())
                                dve.wait_ge(*v.now())
                                nc.vector.tensor_tensor(rg[:, s, p, :], rg[:, s, p, :],
                                                        gt[:, s, 2 * r:2 * r + 2, h], ALU.mult).then_inc(*v.tick())
                                dve.wait_ge(*v.now())
                                for i in range(2):
                                    e = ee[:, s, p * 2 * SEQ + i * SEQ:p * 2 * SEQ + (i + 1) * SEQ]
                                    nc.vector.tensor_scalar(e, e, rg[:, s, p, i:i + 1], None, ALU.mult)\
                                        .then_inc(*v.tick("probs", s, st, k - 1))
                            if k < 2 * H8:
                                dve.wait_ge(*after("scoresF", s, k))
                                nc.vector.tensor_reduce(mx[:, s, k % 2, 0:2], sc[:, s, :, :], AX.X, ALU.max, negate=True)\
                                    .then_inc(*v.tick("maxima", s, k))
                            if k >= 2:
                                h, r = (k - 2) // 2, k % 2
                                dst = big[:, s, (h % 2) * TILES * SEQ:(h % 2 + 1) * TILES * SEQ]\
                                    .rearrange("p (k q) -> p k q", k=TILES)
                                dve.wait_ge(*after("turned probs", s, st, k - 2, 1))
                                nc.vector.tensor_copy(dst[:, :, (2 * r + 1) * P:(2 * r + 2) * P],
                                                      tb[:, s, :].rearrange("p (k q) -> p k q", k=TILES))\
                                    .then_inc(*v.tick())
                                read(s, "t", st, k - 2, 1)
                            yield
                        yield
                        residual(st, s)
                        yield

                    def ternary(st, s):
                        yield from norm(st, s)
                        yield
                        yield
                        yield
                        yield
                        residual(st, s)
                        yield

                    def thread(s):
                        dve.wait_ge(x_in[s], 16)
                        yield from network_of(s, attention, experts, self_attention, ternary)

                    merged(thread)
                    dve.wait_ge(*v.now())

                @block.gpsimd
                def _(pool):
                    g = Progress("pool", plan)

                    def norm(st, s):
                        for again in range(NORM_STEPS[st]):
                            pool.wait_ge(*after("variance", s, st, again))
                            nc.gpsimd.tensor_tensor(rstd[:, s, :], ve[:, s, :], minus_half[:, :], ALU.pow)\
                                .then_inc(*g.tick("rstd", s, st, again))
                            yield
                        yield
                        yield

                    def attention(st, s):
                        first = (turn * THREADS + s) * KEYS
                        n = ATT[st]
                        units = n // H8 * TILES
                        prev = {"X1": "X0", "X2": "X1", "X3": "X2"}.get(st)
                        if prev:
                            pool.wait_ge(*after("values", s, prev, ATT[prev] // H8 * TILES - 2))
                        src = ctxv[st] if st in HEADROWS else small_("ctxT")
                        nc.gpsimd.tensor_copy(ctxb[:, s, :], src[:, bass.ds(first, KEYS)])\
                            .then_inc(*g.tick("ctx cols", s, st))
                        if st in HEADROWS:
                            nc.gpsimd.tensor_tensor(
                                kb[:, s, 0:n * KEYS].rearrange("p (h k) -> p h k", h=n),
                                ctxk[st][:, bass.ds(first, KEYS)].unsqueeze(1).to_broadcast([P, n, KEYS]),
                                headmask[:, :].unsqueeze(2).to_broadcast([P, n, KEYS]), ALU.mult)\
                                .then_inc(*g.tick("keys", s, st))
                        yield from norm(st, s)
                        yield
                        for k in range(units + 2):
                            if 1 <= k <= units:
                                u = k - 1
                                if st == "X2":
                                    pool.wait_ge(*after("exps", s, st, u))
                                    pool.wait_ge(*after("top taken", s, st, u))
                                    taken = wk[:, s, u % 2, :]
                                    nc.gpsimd.tensor_scalar(taken, taken, TAKEN_BELOW, None, ALU.is_le)\
                                        .then_inc(*g.tick())
                                    pool.wait_ge(*g.now())
                                    nc.gpsimd.tensor_tensor(unit(s, u), unit(s, u), taken, ALU.mult)\
                                        .then_inc(*g.tick("masked", s, st, u))
                                    yield
                                pool.wait_ge(*after("rsum", s, st, u))
                                e = unit(s, u).rearrange("p (h k) -> p h k", h=H8)
                                nc.gpsimd.tensor_tensor(
                                    e, e, rs[:, s, u % 2, :].unsqueeze(2).to_broadcast([P, H8, KEYS]), ALU.mult)\
                                    .then_inc(*g.tick("probs", s, st, u))
                            elif st == "X2":
                                yield
                            for _ in range(max(1, SUBSTEPS[st] - 1)):
                                yield
                        yield
                        yield

                    def rest(st, s):
                        yield from norm(st, s)
                        if st == "F1":
                            for k in range(2 + TOPK_STEPS + 1):
                                yield
                            for i in range(E1):
                                pool.wait_ge(*after("hot", s, i))
                                if i >= 2:
                                    pool.wait_ge(*after("hot turned", s, i - 2))
                                nc.gpsimd.tensor_tensor(hotg[s][:, i % 2, :, :], hot[s][:, i % 2, :, :],
                                                        pr[:, s, :, i:i + 1].to_broadcast([P, TILES, P]), ALU.mult)\
                                    .then_inc(*g.tick("hot gated", s, i))
                                yield
                            for k in range(3 + 2):
                                yield
                            return
                        for k in range(STEPS[st] - NORM_STEPS[st] - 2):
                            yield

                    merged(lambda s: network_of(s, attention, rest, rest, rest))
                    pool.wait_ge(*g.now())


def kernel(**inputs):
    import numpy as np
    import concourse.bacc as bacc
    from concourse.bass_utils import run_bass_kernel_spmd

    a = {k: np.asarray(v) for k, v in inputs.items()}
    col = lambda v: np.asarray(v, np.float32).reshape(P, 1)
    vecs = [a["L0_xattn_bq"], a["L0_xattn_bk"], a["L0_xattn_bv"], a["L0_xattn_bo"],
            a["L2_xattn_bq"], a["L2_xattn_bk"], a["L2_xattn_bv"], a["L2_xattn_bo"],
            a["L1_xattn_ln_gamma"], a["L1_xattn_ln_beta"], a["L1_xattn_b_out"], a["L3_xattn_bo"], a["L3_ffn_b2"],
            np.broadcast_to(a["L1_xattn_gate"], (P,))] + list(a["L3_ffn_b1"].reshape(FT, P))
    tiles = lambda w: np.ascontiguousarray(w.reshape(FT, P, D).transpose(1, 0, 2)).reshape(P, FT * D)
    small = np.concatenate(
        [col(v) for v in vecs] + [a["ctx_1024"].reshape(CTX, D).T]
        + [a[f"L{n}_xattn_{w}"].T for n in (0, 2) for w in ("Wq", "Wk", "Wv", "Wo")]
        + [a["L0_ffn_keys"].T, a["L0_ffn_rw"].T, a["L1_ffn_gate_w"].T, a["L2_ffn_Ws"],
           a["L3_ffn_W1"].T, tiles(a["L3_ffn_W2"].T)], axis=1)
    assert small.shape == (P, SMALL_COLS)

    def head_pack(wq, wk, wv, wo, n):
        cut = lambda w: w.reshape(D, n, DH).transpose(2, 1, 0).reshape(DH, n * D)
        return np.stack([cut(wq), cut(wk), cut(wv), wo.reshape(n, DH, D).transpose(1, 0, 2).reshape(DH, n * D)])

    wkv = a["L1_xattn_w_kv"]
    heads1 = head_pack(a["L1_xattn_w_q"], wkv[:, :H16 * DH], wkv[:, H16 * DH:], a["L1_xattn_w_out"], H16)
    heads3 = head_pack(a["L3_xattn_Wq"], a["L3_xattn_Wk"], a["L3_xattn_Wv"], a["L3_xattn_Wo"], H8)
    wkv = a["L2_ffn_Wkv"]
    headsF = head_pack(a["L2_ffn_Wq"], wkv[:, :H8 * DH], wkv[:, H8 * DH:], a["L2_ffn_Wo"].reshape(H8 * DH, D), H8)

    def expert_pack(w1, w2, b1, b2):
        n = w1.shape[0]
        return np.concatenate([w1, b1.reshape(n, FT, P).transpose(0, 2, 1),
                               w2.reshape(n, FT, P, D).transpose(0, 2, 1, 3).reshape(n, P, FT * D), b2.reshape(n, D, 1)], axis=2)

    experts0 = expert_pack(a["L0_ffn_w1"].transpose(0, 2, 1), a["L0_ffn_w2"].transpose(0, 2, 1), a["L0_ffn_b1"],
                           a["L0_ffn_b2"])
    experts1 = expert_pack(a["L1_ffn_w1"], a["L1_ffn_w2"], np.zeros((E1, FT * P), np.float32),
                           np.zeros((E1, D), np.float32))
    rows = np.zeros((1 + H8, D), np.float32)
    rows[0, :E0] = a["L0_ffn_rb"]
    rows[1:] = a["L2_ffn_bo"]
    arrays = {k: np.ascontiguousarray(v) for k, v in dict(
        x=a["x"], small=small, heads1=heads1, heads3=heads3, headsF=headsF, experts0=experts0, experts1=experts1,
        rows=rows).items()}

    plan = Plan()
    for _ in range(2):
        nc = bacc.Bacc("TRN2", target_bir_lowering=False, num_devices=1)
        args = [nc.dram_tensor(f"in_{k}", v.shape, F32, kind="ExternalInput").ap() for k, v in arrays.items()]
        out = nc.dram_tensor("out_x", (BATCH, SEQ, D), F32, kind="ExternalOutput").ap()
        network(nc, plan, *args, out)
    r = run_bass_kernel_spmd(nc, [{f"in_{k}": v for k, v in arrays.items()}], core_ids=[0])
    return r.results[0]["out_x"]
```
